# Optimizing a Trainium2 kernel written in Bass

```python
import numpy as np
import jax
import jax.numpy as jnp

def _softmax(x, axis=-1):
    return jax.nn.softmax(x, axis=axis)

def _gelu(x):
    return jax.nn.gelu(x, approximate=True)

def _silu(x):
    return jax.nn.silu(x)

def _sigmoid(x):
    return jax.nn.sigmoid(x)

def _layernorm(x, axis=-1, eps=1e-05):
    m = jnp.mean(x, axis=axis, keepdims=True)
    v = jnp.var(x, axis=axis, keepdims=True)
    return (x - m) / jnp.sqrt(v + eps)

def _scatter_add(tgt, idx, src, axis=0):
    return tgt.at[idx].add(src)

def _segment_sum(src, seg, n):
    return jax.ops.segment_sum(src, seg, n)
kernel_name = 'mk_adj_resnorm_d4_adj_r2_5f2e8d'

def setup_inputs(seed: int=0):
    np.random.seed(seed)
    _w = jnp.asarray

    def _rec_inputs():
        import jax
        import jax.numpy as jnp
        _gk = jax.random.key(seed)
        x = -0.000929 + 1 * jax.random.normal(jax.random.fold_in(_gk, 1), (4096, 128), jnp.float32)
        _w = (1.0 + jnp.arange(4096, dtype=jnp.float32)) ** (-0.5)
        _w = _w / _w.mean()
        _pij = jnp.clip(0.000488281 * _w[:, None] * _w[None, :], 0.0, 1.0)
        _a = jax.random.uniform(jax.random.fold_in(_gk, 2), (4096, 4096)) < _pij
        _a = jnp.logical_or(_a, jnp.eye(4096, dtype=bool))
        _af = _a.astype(jnp.float32)
        _af = _af * jax.random.uniform(jax.random.fold_in(_gk, 3), (4096, 4096), jnp.float32, 0.05, 1)
        adj = _af
        return (x, adj)
    x, adj = _rec_inputs()

    def _L0_gnn_setup():
        import jax, jax.numpy as jnp
        import numpy as np
        NEG_SLOPE = 0.01
        N_U, N_V = (4096, 4096)
        U_F, V_F = (128, 128)
        HIDS = [128, 128]
        NUM_ROUNDS = 3

        def _glorot(key, fan_in, fan_out):
            lim = np.sqrt(6.0 / (fan_in + fan_out)).astype(np.float32)
            return jax.random.uniform(key, (fan_in, fan_out), jnp.float32, -lim, lim)

        def _mlp(x, W1, b1, W2, b2, W3, b3):
            a = jax.nn.leaky_relu
            x = a(x @ W1 + b1, NEG_SLOPE)
            x = a(x @ W2 + b2, NEG_SLOPE)
            return a(x @ W3 + b3, NEG_SLOPE)
        key = jax.random.key(seed)
        ks = jax.random.split(key, 12)
        inp = {'u_node_feats': jax.random.normal(ks[0], (N_U, U_F), jnp.float32), 'v_node_feats': jax.random.normal(ks[1], (N_V, V_F), jnp.float32), 'uv_adj_mat': jax.random.uniform(ks[2], (N_V, N_U), jnp.float32), 'vu_adj_mat': jax.random.uniform(ks[3], (N_U, N_V), jnp.float32)}
        dims_uv = [U_F] + HIDS + [V_F]
        dims_vu = [V_F] + HIDS + [U_F]
        k = 4
        for tag, dims in (('uv', dims_uv), ('vu', dims_vu)):
            for i in range(3):
                inp[f'{tag}_W{i + 1}'] = _glorot(ks[k], dims[i], dims[i + 1])
                k += 1
                inp[f'{tag}_b{i + 1}'] = jnp.zeros((dims[i + 1],), jnp.float32)
        return inp
    _L0_gnn_all = _L0_gnn_setup()
    _L0_gnn_in = {k: v for k, v in _L0_gnn_all.items() if k in ('v_node_feats', 'uv_W1', 'uv_b1', 'uv_W2', 'uv_b2', 'uv_W3', 'uv_b3', 'vu_W1', 'vu_b1', 'vu_W2', 'vu_b2', 'vu_W3', 'vu_b3')}
    del _L0_gnn_all

    def _L1_gnn_setup():
        import jax, jax.numpy as jnp
        import numpy as np
        N = 4096
        H = 128
        key = jax.random.key(seed)
        k_x, k_A, k_W = jax.random.split(key, 3)
        x = jax.random.normal(k_x, (N, H), dtype=jnp.float32)
        A = jax.random.uniform(k_A, (N, N), dtype=jnp.float32)
        alpha = jnp.array([0.5], dtype=jnp.float32)
        bound = 1.0 / np.sqrt(H)
        W = jax.random.uniform(k_W, (H, H), dtype=jnp.float32, minval=-bound, maxval=bound)
        b = jnp.zeros((H,), dtype=jnp.float32)
        t = jnp.zeros((1,), dtype=jnp.float32)
        return {'t': t, 'x': x, 'A': A, 'alpha': alpha, 'W': W, 'b': b}
    _L1_gnn_all = _L1_gnn_setup()
    _L1_gnn_in = {k: v for k, v in _L1_gnn_all.items() if k in ('t', 'alpha', 'W', 'b')}
    del _L1_gnn_all

    def _L2_gnn_setup():
        import jax, jax.numpy as jnp
        import numpy as np
        N = 8192
        F_IN = 128
        F_OUT = 128
        key = jax.random.key(seed)
        k1, k2, k3, k4 = jax.random.split(key, 4)
        x = jax.random.normal(k1, (N, F_IN), dtype=jnp.float32)
        adj = jax.random.uniform(k2, (N, N), dtype=jnp.float32)
        bound = 1.0 / np.sqrt(2 * F_IN)
        W = jax.random.uniform(k3, (F_OUT, 2 * F_IN), minval=-bound, maxval=bound, dtype=jnp.float32)
        b = jax.random.uniform(k4, (F_OUT,), minval=-bound, maxval=bound, dtype=jnp.float32)
        return {'x': x, 'adj': adj, 'W': W, 'b': b}
    _L2_gnn_all = _L2_gnn_setup()
    _L2_gnn_in = {k: v for k, v in _L2_gnn_all.items() if k in ('W', 'b')}
    del _L2_gnn_all

    def _L3_gnn_setup():
        import jax, jax.numpy as jnp
        import numpy as np
        N, F_DIM, H_DIM = (4096, 128, 128)

        def _gwnn_layer(features, wavelets, wavelets_inv, W, filt):
            xw = features @ W
            spec = wavelets_inv @ xw
            spec = filt[:, None] * spec
            return wavelets @ spec
        key = jax.random.key(seed)
        ks = jax.random.split(key, 7)
        inp = {'input': jax.random.normal(ks[0], (N, F_DIM), dtype=jnp.float32), 'wavelets': jax.random.normal(ks[1], (N, N), dtype=jnp.float32) / np.sqrt(N), 'wavelets_inv': jax.random.normal(ks[2], (N, N), dtype=jnp.float32) / np.sqrt(N), 'W1': jax.random.uniform(ks[3], (F_DIM, H_DIM), dtype=jnp.float32, minval=-np.sqrt(6.0 / (F_DIM + H_DIM)), maxval=np.sqrt(6.0 / (F_DIM + H_DIM))), 'f1': jax.random.uniform(ks[4], (N,), dtype=jnp.float32, minval=0.9, maxval=1.1), 'W2': jax.random.uniform(ks[5], (H_DIM, H_DIM), dtype=jnp.float32, minval=-np.sqrt(6.0 / (H_DIM + H_DIM)), maxval=np.sqrt(6.0 / (H_DIM + H_DIM))), 'f2': jax.random.uniform(ks[6], (N,), dtype=jnp.float32, minval=0.9, maxval=1.1)}
        return inp
    _L3_gnn_all = _L3_gnn_setup()
    _L3_gnn_in = {k: v for k, v in _L3_gnn_all.items() if k in ('W1', 'f1', 'W2', 'f2')}
    del _L3_gnn_all
    return {'x': x, 'adj': adj, 'L0_gnn_v_node_feats': _L0_gnn_in['v_node_feats'], 'L0_gnn_uv_W1': _L0_gnn_in['uv_W1'], 'L0_gnn_uv_b1': _L0_gnn_in['uv_b1'], 'L0_gnn_uv_W2': _L0_gnn_in['uv_W2'], 'L0_gnn_uv_b2': _L0_gnn_in['uv_b2'], 'L0_gnn_uv_W3': _L0_gnn_in['uv_W3'], 'L0_gnn_uv_b3': _L0_gnn_in['uv_b3'], 'L0_gnn_vu_W1': _L0_gnn_in['vu_W1'], 'L0_gnn_vu_b1': _L0_gnn_in['vu_b1'], 'L0_gnn_vu_W2': _L0_gnn_in['vu_W2'], 'L0_gnn_vu_b2': _L0_gnn_in['vu_b2'], 'L0_gnn_vu_W3': _L0_gnn_in['vu_W3'], 'L0_gnn_vu_b3': _L0_gnn_in['vu_b3'], 'L1_gnn_t': _L1_gnn_in['t'], 'L1_gnn_alpha': _L1_gnn_in['alpha'], 'L1_gnn_W': _L1_gnn_in['W'], 'L1_gnn_b': _L1_gnn_in['b'], 'L2_gnn_W': _L2_gnn_in['W'], 'L2_gnn_b': _L2_gnn_in['b'], 'L3_gnn_W1': _L3_gnn_in['W1'], 'L3_gnn_f1': _L3_gnn_in['f1'], 'L3_gnn_W2': _L3_gnn_in['W2'], 'L3_gnn_f2': _L3_gnn_in['f2']}

def reference(x, adj, L0_gnn_v_node_feats, L0_gnn_uv_W1, L0_gnn_uv_b1, L0_gnn_uv_W2, L0_gnn_uv_b2, L0_gnn_uv_W3, L0_gnn_uv_b3, L0_gnn_vu_W1, L0_gnn_vu_b1, L0_gnn_vu_W2, L0_gnn_vu_b2, L0_gnn_vu_W3, L0_gnn_vu_b3, L1_gnn_t, L1_gnn_alpha, L1_gnn_W, L1_gnn_b, L2_gnn_W, L2_gnn_b, L3_gnn_W1, L3_gnn_f1, L3_gnn_W2, L3_gnn_f2):
    import jax
    import jax.numpy as jnp

    def _L0_gnn_ref(u_node_feats, v_node_feats, uv_adj_mat, vu_adj_mat, uv_W1, uv_b1, uv_W2, uv_b2, uv_W3, uv_b3, vu_W1, vu_b1, vu_W2, vu_b2, vu_W3, vu_b3):
        import jax, jax.numpy as jnp
        import numpy as np
        NEG_SLOPE = 0.01
        N_U, N_V = (4096, 4096)
        U_F, V_F = (128, 128)
        HIDS = [128, 128]
        NUM_ROUNDS = 3

        def _glorot(key, fan_in, fan_out):
            lim = np.sqrt(6.0 / (fan_in + fan_out)).astype(np.float32)
            return jax.random.uniform(key, (fan_in, fan_out), jnp.float32, -lim, lim)

        def _mlp(x, W1, b1, W2, b2, W3, b3):
            a = jax.nn.leaky_relu
            x = a(x @ W1 + b1, NEG_SLOPE)
            x = a(x @ W2 + b2, NEG_SLOPE)
            return a(x @ W3 + b3, NEG_SLOPE)
        u, v = (u_node_feats, v_node_feats)
        for _ in range(NUM_ROUNDS):
            v = _mlp(uv_adj_mat @ u, uv_W1, uv_b1, uv_W2, uv_b2, uv_W3, uv_b3)
            u = _mlp(vu_adj_mat @ v, vu_W1, vu_b1, vu_W2, vu_b2, vu_W3, vu_b3)
        return v

    def _L1_gnn_ref(t, x, A, alpha, W, b):
        import jax, jax.numpy as jnp
        import numpy as np
        N = 4096
        H = 128
        a = alpha[0]
        A_prime = a * A
        diag = jnp.diagonal(A_prime) + (1.0 - a)
        A_prime = A_prime.at[jnp.arange(N), jnp.arange(N)].set(diag)
        out_degree = A_prime.sum(axis=1)
        inv_deg = jnp.where(out_degree == 0.0, 0.0, 1.0 / out_degree)
        x = inv_deg[:, None] * A_prime @ x
        x = x @ W.T + b
        return jax.nn.relu(x)

    def _L2_gnn_ref(x, adj, W, b):
        import jax, jax.numpy as jnp
        import numpy as np
        N = 8192
        F_IN = 128
        F_OUT = 128
        neigh = adj @ x
        W_self = W[:, :F_IN]
        W_neigh = W[:, F_IN:]
        return x @ W_self.T + neigh @ W_neigh.T + b

    def _L3_gnn_ref(input, wavelets, wavelets_inv, W1, f1, W2, f2):
        import jax, jax.numpy as jnp
        import numpy as np
        N, F_DIM, H_DIM = (4096, 128, 128)

        def _gwnn_layer(features, wavelets, wavelets_inv, W, filt):
            xw = features @ W
            spec = wavelets_inv @ xw
            spec = filt[:, None] * spec
            return wavelets @ spec
        h1 = jax.nn.relu(_gwnn_layer(input, wavelets, wavelets_inv, W1, f1))
        out = _gwnn_layer(h1, wavelets, wavelets_inv, W2, f2)
        return out
    x = _layernorm(x + _L0_gnn_ref(x, L0_gnn_v_node_feats, adj, adj, L0_gnn_uv_W1, L0_gnn_uv_b1, L0_gnn_uv_W2, L0_gnn_uv_b2, L0_gnn_uv_W3, L0_gnn_uv_b3, L0_gnn_vu_W1, L0_gnn_vu_b1, L0_gnn_vu_W2, L0_gnn_vu_b2, L0_gnn_vu_W3, L0_gnn_vu_b3), axis=-1)
    x = _layernorm(x + _L1_gnn_ref(L1_gnn_t, x, adj, L1_gnn_alpha, L1_gnn_W, L1_gnn_b), axis=-1)
    x = _layernorm(x + _L2_gnn_ref(x, adj, L2_gnn_W, L2_gnn_b), axis=-1)
    x = _layernorm(x + _L3_gnn_ref(x, adj, adj, L3_gnn_W1, L3_gnn_f1, L3_gnn_W2, L3_gnn_f2), axis=-1)
    return x

_drawn_inputs = setup_inputs


def setup_inputs(seed=0):
    import zlib

    import numpy as np

    out = dict(_drawn_inputs(seed))
    spreads = {'L0_gnn_uv_b1': (0.0, 0.1),
     'L0_gnn_uv_b2': (0.0, 0.1),
     'L0_gnn_uv_b3': (0.0, 0.1),
     'L0_gnn_vu_b1': (0.0, 0.1),
     'L0_gnn_vu_b2': (0.0, 0.1),
     'L0_gnn_vu_b3': (0.0, 0.1),
     'L1_gnn_b': (0.0, 0.1)}
    factors = {}
    for name, (base, spread) in spreads.items():
        noise = np.random.default_rng([zlib.crc32(name.encode()), seed]).standard_normal(out[name].shape)
        drawn = base * np.exp(spread * noise) if base else spread * noise
        out[name] = jnp.asarray(drawn.astype(out[name].dtype))
    for name, factor in factors.items():
        out[name] = (out[name] * factor).astype(out[name].dtype)
    return out
```

```python
import numpy as np
import concourse.bass as bass
from concourse import mybir
from contextlib import ExitStack

P = 128
NODES = 4096
FEAT = 128
TILES = NODES // P
CHUNK = 512
CHUNKS = NODES // CHUNK
ROWS = CHUNK // P
GROUP = 4
GROUPS = TILES // GROUP
LATE = TILES - GROUP
RESIDENT = 5
STREAMED = TILES - RESIDENT
SLOT = 3
SLOTS = STREAMED // SLOT
PAIR = 2 * P
NAT = NODES * 2
ASM = STREAMED * PAIR

EPS = 1e-5
SLOPE = 0.01
TOP = 14
EXPONENT = 0x7F800000
MIRROR = float(254 << 23)
SMALLEST = 2.0 ** -111

STAGES = ["uv", "vu", "uv", "vu", "uv_norm", "conv1", "conv2", "filter1", "relu", "filter2", "out"]
LAST = len(STAGES) - 1
MLP = ("uv", "vu", "uv_norm")
CONV = ("conv1", "conv2")
NORM = ("uv_norm", "conv1", "conv2", "out")
MATS = ["uv_W1", "uv_W2", "uv_W3", "vu_W1", "vu_W2", "vu_W3", "L1_WT", "L2_WselfT", "L2_WneighT", "L3_W1", "L3_W2"]
COLS = ["uv_b1", "uv_b2", "vu_b1", "vu_b2"]
ROWVECS = ["uv_b3", "vu_b3", "L1_b", "L2_b"]


def nth(kinds, s, c):
    return CHUNKS * sum(STAGES[r] in kinds for r in range(s)) + c + 1


def everywhere(s, c):
    return CHUNKS * s + c + 1


def build(nc, adj, x, mats, cols, rowvecs, filters, alpha, out):
    f32, f16, bf16, i32 = mybir.dt.float32, mybir.dt.float16, mybir.dt.bfloat16, mybir.dt.int32
    ALU, ACT, AX = mybir.AluOpType, mybir.ActivationFunctionType, mybir.AxisListType
    AMAX = bass.bass_isa.ReduceOp.absmax

    adjT = nc.dram_tensor("adjT", (CHUNKS, SLOTS, P, ROWS * SLOT * PAIR), f16, kind="Internal").ap()
    x3_dram = nc.dram_tensor("x3", (TILES, P, FEAT), f32, kind="Internal").ap()
    adj_v = adj.rearrange("(t p) (h k) -> t h p k", p=P, h=2)
    x_v = x.rearrange("(t p) f -> p t f", p=P)
    out_v = out.rearrange("(t p) f -> t p f", p=P)

    with ExitStack() as ctx:
        def sb(name, shape, dt):
            return ctx.enter_context(nc.sbuf_tensor(name, shape, dt))

        def bank(name):
            return ctx.enter_context(nc.psum_tensor(name, [P, CHUNK], f32))

        def sem(name):
            return ctx.enter_context(nc.semaphore(name))

        home = sb("home", [P, CHUNKS, ROWS, RESIDENT, 2, P], f16)
        region = sb("region", [P, 2 * NAT + 2 * ASM], f16)
        nat = [region[:, b * NAT:(b + 1) * NAT].bitcast(f32) for b in range(2)]
        asm = [region[:, 2 * NAT + b * ASM:2 * NAT + (b + 1) * ASM].rearrange("p (k h n) -> p k h n", h=2, n=P)
               for b in range(2)]
        slot_flat = [region[:, g * ROWS * SLOT * PAIR:(g + 1) * ROWS * SLOT * PAIR] for g in range(SLOTS)]
        slot = [v.rearrange("p (j k h n) -> p j k h n", k=SLOT, h=2, n=P) for v in slot_flat]
        x_parts = sb("x_parts", [P, TILES, 2, FEAT], f16)
        x_f32 = sb("x_f32", [P, TILES, FEAT], f32)
        x_rows = x_f32[:, :, :].rearrange("p t f -> p (t f)")
        undo_row = sb("undo_row", [P, CHUNKS, CHUNK], bf16)
        mat = sb("mat", [P, len(MATS), FEAT], f32)
        kept = sb("kept", [P, FEAT], f32)
        mixed = sb("mixed", [P, FEAT], f32)
        col = sb("col", [P, len(COLS)], f32)
        vec = sb("vec", [P, len(ROWVECS), FEAT], f32)
        filt = sb("filt", [P, 2, TILES], f32)
        alpha_c = sb("alpha_c", [P, 1], f32)
        beta_c = sb("beta_c", [P, 1], f32)
        eps_c = sb("eps_c", [P, 1], f32)
        ident = sb("ident", [P, P], f32)
        ones = sb("ones", [P, P], f32)
        diag = sb("diag", [P, ROWS, P], f32)
        row_max2 = sb("row_max2", [P, 2], f32)
        row_max = sb("row_max", [P, 1], f32)
        row_exp = sb("row_exp", [P, 1], f32)
        row_undo = sb("row_undo", [P, ROWS], f32)
        row_scale = sb("row_scale", [P, ROWS], f32)
        row_sum2 = sb("row_sum2", [P, ROWS, 2], f32)
        row_sum = sb("row_sum", [P, ROWS], f32)
        degree = sb("degree", [P, TILES], f32)
        nonzero = sb("nonzero", [P, TILES], f32)
        inv_degree = sb("inv_degree", [P, TILES], f32)
        chunk_max = sb("chunk_max", [P, CHUNKS], f32)
        part_max = sb("part_max", [P, 1], f32)
        all_max = sb("all_max", [P, 1], f32)
        x_exp = sb("x_exp", [P, 1], f32)
        x_scale = sb("x_scale", [P, 2, 2], f32)
        x_undo = sb("x_undo", [P, 2, 2], f32)
        early = sb("early", [P, CHUNK], f32)
        zsum = sb("zsum", [P, CHUNK], f32)
        z = sb("z", [P, CHUNK], f32)
        biased = sb("biased", [P, CHUNK], f32)
        h1 = sb("h1", [P, CHUNK], f32)
        h2 = sb("h2", [P, CHUNK], f32)
        x_now = h2[:, :].rearrange("p (j f) -> p j f", j=ROWS)
        y = sb("y", [P, ROWS, FEAT], f32)
        ysum = biased[:, :].rearrange("p (j f) -> p j f", j=ROWS)
        stats = sb("stats", [P, ROWS, 6], f32)
        apart = sb("apart", [P, ROWS], f32)
        twice_mean = sb("twice_mean", [P, ROWS], f32)
        mean = sb("mean", [P, ROWS], f32)
        within = sb("within", [P, ROWS], f32)
        between = sb("between", [P, ROWS], f32)
        spread = sb("spread", [P, ROWS], f32)
        std = sb("std", [P, ROWS], f32)
        rstd = sb("rstd", [P, ROWS], f32)

        acc_early, acc_late = bank("acc_early"), bank("acc_late")
        turned = [bank(f"turned{i}") for i in range(4)]
        m0, m1 = bank("m0"), bank("m1")

        s_x = sem("x_loaded")
        s_w = sem("weights_loaded")
        s_const = sem("constants_ready")
        s_ident = sem("identity_zeroed")
        s_nat = [[sem(f"nat{b}{h}_loaded") for h in range(2)] for b in range(2)]
        s_stored = [sem(f"asm{b}_stored") for b in range(2)]
        s_slot = [sem(f"slot{g}_loaded") for g in range(SLOTS)]
        s_rmax2 = sem("row_half_max")
        s_rmax = sem("row_max_ready")
        s_rexp = sem("row_exponent_ready")
        s_rundo = sem("row_undo_ready")
        s_rscale = sem("row_scale_ready")
        s_scaled = sem("row_half_scaled")
        s_turned = sem("blocks_transposed")
        s_head = sem("head_written")
        s_tail = sem("tail_written_and_bank_free")
        s_diag = sem("diagonal_ready")
        s_bcast = sem("row_undo_broadcast")
        s_undo = sem("undo_row_ready")
        s_rsum = sem("row_sum_ready")
        s_deg = sem("degree_ready")
        s_setup = sem("setup_step")
        s_group = sem("group_multiplied")
        s_early = sem("early_read")
        s_zsum = sem("late_read")
        s_z = sem("z_ready")
        s_mm1 = sem("layer1_multiplied")
        s_biased1 = sem("layer1_biased")
        s_h1 = sem("h1_ready")
        s_mm2 = sem("layer2_multiplied")
        s_biased2 = sem("layer2_biased")
        s_h2 = sem("h2_ready")
        s_xnow = sem("x_now_copied")
        s_xt = sem("x_transposed")
        s_xtc = sem("x_transposed_copied")
        s_lin = sem("linear_done")
        s_linread = sem("linear_read")
        s_y = sem("y_ready")
        s_ysum = sem("y_sum_ready")
        s_stats = sem("stats_ready")
        s_apart = sem("apart_ready")
        s_within = sem("within_ready")
        s_between = sem("between_ready")
        s_mv = sem("mean_and_spread_ready")
        s_std = sem("std_ready")
        s_rstd = sem("rstd_ready")
        s_new = sem("new_x_ready")
        s_cmax = sem("chunk_max_ready")
        s_pmax = sem("partition_max_ready")
        s_amax = sem("all_max_ready")
        s_xexp = sem("x_exponent_ready")
        s_xundo = sem("x_undo_ready")
        s_xscale = sem("x_scale_ready")
        s_xhead = sem("x_head_ready")
        s_xtail = sem("x_parts_ready")
        s_reload = sem("residual_reloaded")
        s_spill = sem("x3_spilled")
        s_out = sem("out_stored")

        block = ctx.enter_context(nc.Block())

        def m(name):
            return mat[:, MATS.index(name), :]

        def column(name):
            return col[:, COLS.index(name):COLS.index(name) + 1]

        def per_row(name):
            return vec[:, ROWVECS.index(name), :].unsqueeze(1).to_broadcast([P, ROWS, FEAT])

        def rows(c):
            return slice(c * ROWS, (c + 1) * ROWS) if isinstance(c, int) else bass.ds(c * ROWS, ROWS)

        def tiles3(psum):
            return psum[:, :].rearrange("p (j n) -> p j n", j=ROWS)

        def places(c, j, q):
            k0, k1 = GROUP * q, GROUP * (q + 1)
            if k0 < RESIDENT:
                n = min(k1, RESIDENT) - k0
                yield 0, n, home[:, c, j, k0:k0 + n, :, :]
            if k1 > RESIDENT:
                a = max(k0, RESIDENT)
                yield a - k0, k1 - a, asm[j % 2][:, a - RESIDENT:k1 - RESIDENT, :, :]

        def x_count(s, late):
            return 1 if s == 0 else 2 * s + late

        def scale_at(table, s, late):
            late = late if s else 0
            return table[:, s % 2, late:late + 1]

        @block.sync
        def _(sp):
            sp.dma_start(nat[0][:, 0:NODES // 2], adj_v[0, 0]).then_inc(s_nat[0][0], 16)
            sp.dma_start(nat[0][:, NODES // 2:], adj_v[0, 1]).then_inc(s_nat[0][1], 16)
            sp.dma_start(x_f32[:, :, :], x_v).then_inc(s_x, 16)
            sp.dma_start(nat[1][:, 0:NODES // 2], adj_v[1, 0]).then_inc(s_nat[1][0], 16)
            sp.dma_start(nat[1][:, NODES // 2:], adj_v[1, 1]).then_inc(s_nat[1][1], 16)

            def load(c, j):
                for h in range(2):
                    sp.wait_ge(s_turned, GROUPS * (c * ROWS + j) + GROUPS // 2 * (h + 1))
                    sp.dma_start(nat[j % 2][:, h * NODES // 2:(h + 1) * NODES // 2],
                                 adj_v[c * ROWS + j + 2, h]).then_inc(s_nat[j % 2][h], 16)

            def store(c, j):
                sp.wait_ge(s_tail, 4 + GROUPS * (c * ROWS + j + 1))
                sp.dma_start(
                    adjT[c, :, :, j * SLOT * PAIR:(j + 1) * SLOT * PAIR].rearrange("g p e -> p g e"),
                    asm[j % 2].rearrange("p (g k) h n -> p g (k h n)", g=SLOTS),
                ).then_inc(s_stored[j % 2], 16)

            with sp.Fori(0, CHUNKS - 1) as c:
                for j in range(ROWS):
                    load(c, j)
                    store(c, j)
            for j in range(ROWS):
                if j < 2:
                    load(CHUNKS - 1, j)
                store(CHUNKS - 1, j)
            sp.wait_ge(s_group, GROUPS * CHUNKS)
            for b in range(2):
                sp.wait_ge(s_stored[b], 16 * TILES // 2)
            with sp.Fori(1, LAST + 1) as s:
                with sp.Fori(0, CHUNKS) as c:
                    for g in range(SLOTS):
                        last_group = (RESIDENT + SLOT * (g + 1) - 1) // GROUP
                        sp.wait_ge(s_group, s * (GROUPS * CHUNKS) + c * GROUPS - GROUPS + last_group + 1)
                        sp.dma_start(slot_flat[g], adjT[c, g]).then_inc(s_slot[g], 16)

        @block.gpsimd
        def _(pool):
            nc.gpsimd.memset(ident[:, :], 0.0).then_inc(s_ident, 1)
            nc.gpsimd.memset(ones[:, :], 1.0)
            nc.gpsimd.memset(eps_c[:, :], EPS)
            pool.wait_ge(s_ident, 1)
            nc.gpsimd.affine_select(out=ident[:, :], in_=ident[:, :], compare_op=ALU.not_equal, fill=1.0, base=0,
                                    pattern=[[-1, P]], channel_multiplier=1).then_inc(s_const, 1)

            def reduce_max(s, late):
                pool.wait_ge(s_pmax, x_count(s, late))
                nc.gpsimd.partition_all_reduce(all_max[:, :], part_max[:, :], P, AMAX).then_inc(s_amax, 1)

            def reload(s, source):
                for c in range(CHUNKS):
                    pool.wait_ge(s_xtail, CHUNKS * s + c + 1)
                    pool.dma_start(x_f32[:, c * ROWS:(c + 1) * ROWS, :],
                                   source[:, c * ROWS:(c + 1) * ROWS, :]).then_inc(s_reload, 16)

            def write_rows(s, c, dest, done):
                pool.wait_ge(s_new, everywhere(s, c))
                pool.dma_start(dest[rows(c), :, :].rearrange("t p f -> p t f"), x_f32[:, rows(c), :]).then_inc(done, 16)

            reduce_max(0, 0)
            for s in range(LAST + 1):
                if STAGES[s] == "uv_norm":
                    reload(s, x_v)
                if STAGES[s] == "out":
                    pool.wait_ge(s_spill, 16 * CHUNKS)
                    reload(s, x3_dram.rearrange("t p f -> p t f"))
                for c in range(CHUNKS):
                    if STAGES[s] == "conv2":
                        write_rows(s, c, x3_dram, s_spill)
                    if STAGES[s] == "out":
                        write_rows(s, c, out_v, s_out)
                    if s < LAST and c >= CHUNKS - 2:
                        reduce_max(s + 1, int(c == CHUNKS - 1))
            pool.wait_ge(s_out, 16 * CHUNKS)

        @block.scalar
        def _(act):
            act.dma_start(mat[:, :, :], mats.rearrange("m p f -> p m f")).then_inc(s_w, 16)
            act.dma_start(col[:, :], cols).then_inc(s_w, 16)
            act.dma_start(vec[:, :, :], rowvecs.unsqueeze(0).to_broadcast([P, len(ROWVECS), FEAT])).then_inc(s_w, 16)
            act.dma_start(filt[:, :, :], filters.rearrange("a p t -> p a t")).then_inc(s_w, 16)
            act.dma_start(alpha_c[:, :], alpha.to_broadcast([P, 1])).then_inc(s_w, 16)

            def scale_half(t, j, h):
                act.wait_ge(s_rscale, t + 1)
                half = nat[j % 2][:, h * NODES // 2:(h + 1) * NODES // 2]
                nc.scalar.activation(half, half, ACT.Copy, scale=row_scale[:, j:j + 1],
                                     accum_out=row_sum2[:, j, h:h + 1]).then_inc(s_scaled, 1)

            def head(c, j, q):
                act.wait_ge(s_turned, GROUPS * (c * ROWS + j) + q + 1)
                if GROUP * (q + 1) > RESIDENT and q < 2:
                    act.wait_ge(s_stored[j % 2], 16 * (c * (ROWS // 2) + j // 2))
                for a, n, dest in places(c, j, q):
                    last = nc.scalar.activation(dest[:, :, 0, :],
                                                turned[q % 4][:, a * P:(a + n) * P].rearrange("p (k n) -> p k n", n=P),
                                                ACT.Copy)
                last.then_inc(s_head, 1)

            def read_early(s, c):
                act.wait_ge(s_group, GROUPS * everywhere(s, c) - 1)
                if s or not (isinstance(c, int) and c == 0):
                    act.wait_ge(s_zsum, everywhere(s, c) - 1)
                nc.scalar.activation(early[:, :], acc_early[:, :], ACT.Copy,
                                     scale=scale_at(x_undo, s, 0)).then_inc(s_early, 1)

            def hidden1(s, c):
                act.wait_ge(s_mm1, nth(MLP, s, c))
                nc.scalar.activation(biased[:, :], m0[:, :], ACT.Identity,
                                     bias=column(STAGES[s][:2] + "_b1")).then_inc(s_biased1, 1)

            def hidden2(s, c):
                act.wait_ge(s_mm2, nth(MLP, s, c))
                nc.scalar.activation(biased[:, :], m1[:, :], ACT.Identity,
                                     bias=column(STAGES[s][:2] + "_b2")).then_inc(s_biased2, 1)

            def after(s, c):
                if STAGES[s] in MLP:
                    hidden1(s, c)
                    hidden2(s, c)
                if STAGES[s] in CONV:
                    act.wait_ge(s_lin, everywhere(s, c) - 1)
                    nc.scalar.activation(x_now[:, :, :], x_f32[:, rows(c), :], ACT.Copy).then_inc(s_xnow, 1)
                    act.wait_ge(s_xt, nth(CONV, s, c))
                    nc.scalar.activation(h1[:, :], m1[:, :], ACT.Copy).then_inc(s_xtc, 1)
                if STAGES[s] in NORM:
                    act.wait_ge(s_mv, nth(NORM, s, c))
                    nc.scalar.activation(std[:, :], spread[:, :], ACT.Sqrt, bias=eps_c[:, 0:1],
                                     scale=1.0 / FEAT).then_inc(s_std, 1)

            def x_head(s, b):
                act.wait_ge(s_xscale, x_count(s, int(b == GROUPS - 1)))
                if s:
                    act.wait_ge(s_group, GROUPS * CHUNKS * s - GROUPS + b + 1)
                nc.scalar.activation(x_parts[:, b * GROUP:(b + 1) * GROUP, 0, :], x_f32[:, b * GROUP:(b + 1) * GROUP, :],
                                     ACT.Copy, scale=scale_at(x_scale, s, int(b == GROUPS - 1))).then_inc(s_xhead, 1)

            act.wait_ge(s_w, 16 * 5)
            act.wait_ge(s_const, 1)
            for b in range(GROUPS):
                x_head(0, b)
            for h in range(2):
                scale_half(0, 0, h)

            def chunk0(c, first, final):
                for j in range(ROWS):
                    t_next = c * ROWS + j + 1
                    ahead = not (final and j == ROWS - 1)
                    for q in range(GROUPS):
                        head(c, j, q)
                        if q == 1 and j == 0 and not first:
                            read_early(0, c - 1)
                        if q == 2 and j == 1 and not first:
                            hidden1(0, c - 1)
                        if q == 2 and j == 2 and not first:
                            hidden2(0, c - 1)
                        if q == 5 and ahead:
                            scale_half(t_next, (j + 1) % ROWS, 0)
                    if ahead:
                        scale_half(t_next, (j + 1) % ROWS, 1)

            chunk0(0, True, False)
            with act.Fori(1, CHUNKS - 1) as c:
                chunk0(c, False, False)
            chunk0(CHUNKS - 1, False, True)
            for b in range(GROUPS - 1):
                x_head(1, b)
            read_early(0, CHUNKS - 1)
            after(0, CHUNKS - 1)
            x_head(1, GROUPS - 1)

            for s in range(1, LAST + 1):
                with act.Fori(0, CHUNKS - 1) as c:
                    read_early(s, c)
                    after(s, c)
                if s < LAST:
                    for b in range(GROUPS - 1):
                        x_head(s + 1, b)
                read_early(s, CHUNKS - 1)
                after(s, CHUNKS - 1)
                if s < LAST:
                    x_head(s + 1, GROUPS - 1)

        @block.vector
        def _(dve):
            nc.vector.memset(chunk_max[:, :], 0.0).then_inc(s_tail, 4)

            def power_of_two(largest, exponent, undo, scale, s_exp, s_und, s_sc, n):
                nc.vector.tensor_scalar(exponent.bitcast(i32), largest.bitcast(i32), EXPONENT, None,
                                        ALU.bitwise_and).then_inc(s_exp, 1)
                dve.wait_ge(s_exp, n)
                nc.vector.tensor_scalar(undo, exponent, SMALLEST, 2.0 ** -TOP, ALU.max, ALU.mult).then_inc(s_und, 1)
                dve.wait_ge(s_und, n)
                nc.vector.tensor_scalar(scale.bitcast(i32), undo.bitcast(i32), -1.0, MIRROR,
                                        ALU.mult, ALU.add).then_inc(s_sc, 1)

            def row_half_max(c, j, h, t):
                dve.wait_ge(s_nat[j % 2][h], 16 * (c * (ROWS // 2) + j // 2 + 1))
                nc.vector.tensor_reduce(row_max2[:, h:h + 1], nat[j % 2][:, h * NODES // 2:(h + 1) * NODES // 2],
                                        axis=AX.X, op=ALU.max, apply_absolute_value=True).then_inc(s_rmax2, 1)

            def row_scales(c, j, t, first):
                dve.wait_ge(s_rmax2, 2 * (t + 1))
                nc.vector.tensor_reduce(row_max[:, :], row_max2[:, :], axis=AX.X, op=ALU.max).then_inc(s_rmax, 1)
                dve.wait_ge(s_rmax, t + 1)
                power_of_two(row_max[:, :], row_exp[:, :], row_undo[:, j:j + 1], row_scale[:, j:j + 1],
                             s_rexp, s_rundo, s_rscale, t + 1)
                if j == 0 and not first:
                    dve.wait_ge(s_bcast, c)
                nc.vector.tensor_scalar(diag[:, j, :], ident[:, :], row_undo[:, j:j + 1], None,
                                        ALU.mult).then_inc(s_diag, 1)

            def tail(c, j, q):
                dve.wait_ge(s_head, GROUPS * (c * ROWS + j) + q + 1)
                parts = list(places(c, j, q))
                for a, n, dest in parts:
                    last = nc.vector.tensor_tensor(dest[:, :, 1, :],
                                                   turned[q % 4][:, a * P:(a + n) * P].rearrange("p (k n) -> p k n", n=P),
                                                   dest[:, :, 0, :], ALU.subtract)
                last.then_inc(s_tail, 1)

            def sum_products(s, c):
                n = everywhere(s, c)
                dve.wait_ge(s_group, GROUPS * n)
                dve.wait_ge(s_early, n)
                nc.vector.scalar_tensor_tensor(zsum[:, :], acc_late[:, :], scale_at(x_undo, s, 1), early[:, :],
                                               ALU.mult, ALU.add).then_inc(s_zsum, 1)
                dve.wait_ge(s_zsum, n)
                if s or not (isinstance(c, int) and c == 0):
                    dve.wait_ge(s_lin, n - 1)
                nc.vector.tensor_tensor(z[:, :], zsum[:, :], undo_row[:, c, :], ALU.mult).then_inc(s_z, 1)

            def leaky(s, c, s_biased, h, s_h):
                dve.wait_ge(s_biased, nth(MLP, s, c))
                nc.vector.scalar_tensor_tensor(h[:, :], biased[:, :], SLOPE, biased[:, :],
                                               ALU.mult, ALU.max).then_inc(s_h, 1)

            def hidden(s, c):
                if STAGES[s] in MLP:
                    leaky(s, c, s_biased1, h1, s_h1)
                    leaky(s, c, s_biased2, h2, s_h2)

            def finish(s, c):
                kind = STAGES[s]
                n = everywhere(s, c)
                x_c = x_f32[:, rows(c), :]
                lin = tiles3(m0)
                dve.wait_ge(s_lin, n)
                if kind == "filter1":
                    dve.wait_ge(s_spill, 16 * CHUNKS)
                if kind in ("uv_norm", "out"):
                    dve.wait_ge(s_reload, 16 * CHUNKS * (1 + (kind == "out")))
                if kind in MLP:
                    nc.vector.tensor_tensor(y[:, :, :], lin, per_row(kind[:2] + "_b3"), ALU.add).then_inc(s_linread, 1)
                    dve.wait_ge(s_linread, n)
                    if kind == "uv_norm":
                        nc.vector.scalar_tensor_tensor(ysum[:, :, :], y[:, :, :], SLOPE, y[:, :, :],
                                                       ALU.mult, ALU.max).then_inc(s_y, 1)
                        dve.wait_ge(s_y, nth(("uv_norm", "conv1"), s, c))
                        nc.vector.tensor_tensor(y[:, :, :], ysum[:, :, :], x_c, ALU.add).then_inc(s_ysum, 1)
                    else:
                        nc.vector.scalar_tensor_tensor(x_c, y[:, :, :], SLOPE, y[:, :, :],
                                                       ALU.mult, ALU.max).then_inc(s_new, 1)
                elif kind == "conv1":
                    inv = inv_degree[:, rows(c)].unsqueeze(2).to_broadcast([P, ROWS, FEAT])
                    nc.vector.tensor_tensor(ysum[:, :, :], lin, inv, ALU.mult).then_inc(s_linread, 1)
                    dve.wait_ge(s_linread, n)
                    nc.vector.tensor_tensor(ysum[:, :, :], ysum[:, :, :], per_row("L1_b"), ALU.add).then_inc(s_y, 1)
                    dve.wait_ge(s_y, nth(("uv_norm", "conv1"), s, c))
                    nc.vector.scalar_tensor_tensor(y[:, :, :], ysum[:, :, :], 0.0, x_c,
                                                   ALU.max, ALU.add).then_inc(s_ysum, 1)
                elif kind == "conv2":
                    nc.vector.tensor_tensor(ysum[:, :, :], lin, per_row("L2_b"), ALU.add).then_inc(s_linread, 1)
                    dve.wait_ge(s_linread, n)
                    nc.vector.tensor_tensor(y[:, :, :], ysum[:, :, :], x_c, ALU.add).then_inc(s_ysum, 1)
                elif kind in ("filter1", "filter2"):
                    f = filt[:, int(kind == "filter2"), rows(c)].unsqueeze(2).to_broadcast([P, ROWS, FEAT])
                    nc.vector.tensor_tensor(x_c, lin, f, ALU.mult).then_inc(s_new, 1)
                elif kind == "relu":
                    nc.vector.tensor_scalar(x_c, lin, 0.0, None, ALU.max).then_inc(s_new, 1)
                else:
                    nc.vector.tensor_tensor(y[:, :, :], lin, x_c, ALU.add).then_inc(s_ysum, 1)
                if kind in NORM:
                    k = nth(NORM, s, c)
                    dve.wait_ge(s_ysum, k)
                    for j in range(ROWS):
                        last = nc.vector.bn_stats(stats[:, j, :], y[:, j, :])
                    last.then_inc(s_stats, 1)
                    dve.wait_ge(s_stats, k)
                    nc.vector.tensor_tensor(apart[:, :], stats[:, :, 1], stats[:, :, 4], ALU.subtract).then_inc(s_apart, 1)
                    nc.vector.tensor_tensor(twice_mean[:, :], stats[:, :, 1], stats[:, :, 4], ALU.add)
                    nc.vector.tensor_tensor(within[:, :], stats[:, :, 2], stats[:, :, 5], ALU.add).then_inc(s_within, 1)
                    dve.wait_ge(s_apart, k)
                    nc.vector.scalar_tensor_tensor(between[:, :], apart[:, :], FEAT / 4.0, apart[:, :],
                                                   ALU.mult, ALU.mult).then_inc(s_between, 1)
                    dve.wait_ge(s_within, k)
                    nc.vector.tensor_scalar(mean[:, :], twice_mean[:, :], 0.5, None, ALU.mult)
                    dve.wait_ge(s_between, k)
                    nc.vector.tensor_tensor(spread[:, :], within[:, :], between[:, :], ALU.add).then_inc(s_mv, 1)
                    dve.wait_ge(s_std, k)
                    nc.vector.reciprocal(rstd[:, :], std[:, :]).then_inc(s_rstd, 1)
                    dve.wait_ge(s_rstd, k)
                    for j in range(ROWS):
                        x_j = x_f32[:, c * ROWS + j, :]
                        last = nc.vector.tensor_scalar(x_j, y[:, j, :], mean[:, j:j + 1], rstd[:, j:j + 1],
                                                       ALU.subtract, ALU.mult)
                    last.then_inc(s_new, 1)
                if s < LAST:
                    dve.wait_ge(s_new, n)
                    nc.vector.tensor_reduce(chunk_max[:, bass.ds(c, 1)] if not isinstance(c, int) else
                                            chunk_max[:, c:c + 1], x_c, axis=AX.XY, op=ALU.max,
                                            apply_absolute_value=True).then_inc(s_cmax, 1)

            def x_scales(s, late):
                n = x_count(s, late)
                if s == 0:
                    nc.vector.tensor_reduce(part_max[:, :], x_rows, axis=AX.X, op=ALU.max,
                                            apply_absolute_value=True).then_inc(s_pmax, 1)
                else:
                    dve.wait_ge(s_cmax, everywhere(s - 1, CHUNKS - 1 if late else CHUNKS - 2))
                    src = chunk_max[:, CHUNKS - 1:CHUNKS] if late else chunk_max[:, 0:CHUNKS - 1]
                    nc.vector.tensor_reduce(part_max[:, :], src, axis=AX.X, op=ALU.max).then_inc(s_pmax, 1)
                dve.wait_ge(s_amax, n)
                at = late if s else 0
                power_of_two(all_max[:, :], x_exp[:, :], x_undo[:, s % 2, at:at + 1], x_scale[:, s % 2, at:at + 1],
                             s_xexp, s_xundo, s_xscale, n)
                dve.wait_ge(s_xscale, n)

            def x_tail(s, b):
                dve.wait_ge(s_xhead, GROUPS * s + b + 1)
                nc.vector.scalar_tensor_tensor(x_parts[:, b * GROUP:(b + 1) * GROUP, 1, :],
                                               x_f32[:, b * GROUP:(b + 1) * GROUP, :],
                                               scale_at(x_scale, s, int(b == GROUPS - 1)),
                                               x_parts[:, b * GROUP:(b + 1) * GROUP, 0, :],
                                               ALU.mult, ALU.subtract).then_inc(s_xtail, 1)

            dve.wait_ge(s_x, 16)
            x_scales(0, 0)
            for b in range(GROUPS):
                x_tail(0, b)
            dve.wait_ge(s_const, 1)
            for h in range(2):
                row_half_max(0, 0, h, 0)
            row_scales(0, 0, 0, True)

            def chunk0(c, first, final):
                for j in range(ROWS):
                    jn, cn, t_next = (j + 1) % ROWS, c + (j + 1) // ROWS, c * ROWS + j + 1
                    ahead = not (final and j == ROWS - 1)
                    for q in range(GROUPS):
                        tail(c, j, q)
                        if q == 0 and j == ROWS - 1:
                            dve.wait_ge(s_bcast, c + 1)
                            nc.vector.tensor_copy(undo_row[:, c, :], m1[:, :]).then_inc(s_undo, 1)
                            dve.wait_ge(s_scaled, 2 * ROWS * (c + 1))
                            nc.vector.tensor_tensor(row_sum[:, :], row_sum2[:, :, 0], row_sum2[:, :, 1],
                                                    ALU.add).then_inc(s_rsum, 1)
                            dve.wait_ge(s_rsum, c + 1)
                            nc.vector.tensor_tensor(degree[:, rows(c)], row_sum[:, :], row_undo[:, :], ALU.mult).then_inc(s_deg, 1)
                        if q == 1 and j == 0 and not first:
                            dve.wait_ge(s_undo, c)
                            sum_products(0, c - 1)
                        if q == 4 and j == 1 and not first:
                            leaky(0, c - 1, s_biased1, h1, s_h1)
                        if q == 4 and j == 2 and not first:
                            leaky(0, c - 1, s_biased2, h2, s_h2)
                        if q == 1 and j == 3 and not first:
                            finish(0, c - 1)
                        if q == 1 and ahead:
                            row_half_max(cn, jn, 0, t_next)
                        if q == 4 and ahead:
                            row_half_max(cn, jn, 1, t_next)
                            row_scales(cn, jn, t_next, False)

            chunk0(0, True, False)
            with dve.Fori(1, CHUNKS - 1) as c:
                chunk0(c, False, False)
            chunk0(CHUNKS - 1, False, True)
            x_scales(1, 0)
            for b in range(GROUPS - 1):
                x_tail(1, b)
            dve.wait_ge(s_undo, CHUNKS)
            sum_products(0, CHUNKS - 1)
            hidden(0, CHUNKS - 1)
            finish(0, CHUNKS - 1)
            x_scales(1, 1)
            x_tail(1, GROUPS - 1)

            steps = [0]

            def setup(instruction):
                steps[0] += 1
                instruction.then_inc(s_setup, 1)
                dve.wait_ge(s_setup, steps[0])

            dve.wait_ge(s_w, 16 * 5)
            dve.wait_ge(s_deg, CHUNKS)
            setup(nc.vector.tensor_scalar(beta_c[:, :], alpha_c[:, :], -1.0, 1.0, ALU.mult, ALU.add))
            setup(nc.vector.tensor_scalar(mixed[:, :], m("L1_WT"), alpha_c[:, 0:1], None, ALU.mult))
            setup(nc.vector.tensor_scalar(kept[:, :], m("L1_WT"), beta_c[:, 0:1], None, ALU.mult))
            setup(nc.vector.tensor_scalar(degree[:, :], degree[:, :], alpha_c[:, 0:1], beta_c[:, 0:1],
                                          ALU.mult, ALU.add))
            setup(nc.vector.tensor_scalar(nonzero[:, :], degree[:, :], 0.0, None, ALU.is_equal))
            setup(nc.vector.tensor_tensor(degree[:, :], degree[:, :], nonzero[:, :], ALU.add))
            setup(nc.vector.tensor_scalar(nonzero[:, :], nonzero[:, :], -1.0, 1.0, ALU.mult, ALU.add))
            setup(nc.vector.reciprocal(inv_degree[:, :], degree[:, :]))
            setup(nc.vector.tensor_tensor(inv_degree[:, :], inv_degree[:, :], nonzero[:, :], ALU.mult))

            for s in range(1, LAST + 1):
                with dve.Fori(0, CHUNKS - 1) as c:
                    sum_products(s, c)
                    hidden(s, c)
                    finish(s, c)
                if s < LAST:
                    x_scales(s + 1, 0)
                    for b in range(GROUPS - 1):
                        x_tail(s + 1, b)
                sum_products(s, CHUNKS - 1)
                hidden(s, CHUNKS - 1)
                finish(s, CHUNKS - 1)
                if s < LAST:
                    x_scales(s + 1, 1)
                    x_tail(s + 1, GROUPS - 1)

        @block.tensor
        def _(pe):
            def multiply(k, head_and_tail, early_to, late_to):
                to = early_to if k < LATE else late_to
                head, tail = head_and_tail
                first, last = k in (0, LATE), k in (LATE - 1, TILES - 1)
                nc.tensor.matmul(to, x_parts[:, k, 0, :], head, start=first, stop=False)
                nc.tensor.matmul(to, x_parts[:, k, 0, :], tail, start=False, stop=False)
                return nc.tensor.matmul(to, x_parts[:, k, 1, :], head, start=False, stop=last)

            def free_m0(s, c):
                if s or not (isinstance(c, int) and c == 0):
                    pe.wait_ge(s_new, everywhere(s, c) - 1)

            def step(s, c, k):
                kind = STAGES[s]
                if kind in MLP:
                    w = kind[:2]
                    if k == 0:
                        pe.wait_ge(s_z, everywhere(s, c))
                        free_m0(s, c)
                        nc.tensor.matmul(m0[:, :], m(w + "_W1"), z[:, :], start=True, stop=True).then_inc(s_mm1, 1)
                    if k == 1:
                        pe.wait_ge(s_h1, nth(MLP, s, c))
                        if s == 0:
                            pe.wait_ge(s_undo, c + 1)
                        nc.tensor.matmul(m1[:, :], m(w + "_W2"), h1[:, :], start=True, stop=True).then_inc(s_mm2, 1)
                    if k == 2:
                        pe.wait_ge(s_h2, nth(MLP, s, c))
                        for j in range(ROWS):
                            last = nc.tensor.matmul(m0[:, j * P:(j + 1) * P], h2[:, j * P:(j + 1) * P], m(w + "_W3"),
                                                    start=True, stop=True)
                        last.then_inc(s_lin, 1)
                    return
                if kind in CONV:
                    if k == 0:
                        pe.wait_ge(s_xnow, nth(CONV, s, c))
                        for j in range(ROWS):
                            last = nc.tensor.transpose(m1[:, j * P:(j + 1) * P], x_now[:, j, :], ident[:, :])
                        last.then_inc(s_xt, 1)
                    if k == 1:
                        own, neigh = (kept[:, :], mixed[:, :]) if kind == "conv1" else (m("L2_WselfT"), m("L2_WneighT"))
                        pe.wait_ge(s_z, everywhere(s, c))
                        pe.wait_ge(s_xtc, nth(CONV, s, c))
                        free_m0(s, c)
                        for j in range(ROWS):
                            nc.tensor.matmul(m0[:, j * P:(j + 1) * P], z[:, j * P:(j + 1) * P], neigh,
                                             start=True, stop=False)
                            last = nc.tensor.matmul(m0[:, j * P:(j + 1) * P], h1[:, j * P:(j + 1) * P], own,
                                                    start=False, stop=True)
                        last.then_inc(s_lin, 1)
                    return
                if k == 0:
                    pe.wait_ge(s_z, everywhere(s, c))
                    free_m0(s, c)
                    for j in range(ROWS):
                        z_j, to = z[:, j * P:(j + 1) * P], m0[:, j * P:(j + 1) * P]
                        if kind in ("relu", "out"):
                            last = nc.tensor.transpose(to, z_j, ident[:, :])
                        else:
                            last = nc.tensor.matmul(to, z_j, m("L3_W1" if kind == "filter1" else "L3_W2"),
                                                    start=True, stop=True)
                    last.then_inc(s_lin, 1)

            def transpose_group(c, j, q):
                u = GROUPS * (c * ROWS + j) + q
                pe.wait_ge(s_scaled, 2 * (c * ROWS + j) + 1 + q // (GROUPS // 2))
                pe.wait_ge(s_tail, u + 1)
                for i in range(GROUP):
                    k = GROUP * q + i
                    last = nc.tensor.transpose(turned[q % 4][:, i * P:(i + 1) * P], nat[j % 2][:, k * P:(k + 1) * P],
                                               ident[:, :])
                last.then_inc(s_turned, 1)

            def multiply_group(c, j, q, first):
                pe.wait_ge(s_tail, 4 + GROUPS * (c * ROWS + j) + q + 1)
                if j == 0 and q == 0 and not first:
                    pe.wait_ge(s_early, c)
                if j == 0 and q == GROUPS - 1 and not first:
                    pe.wait_ge(s_zsum, c)
                for a, n, src in places(c, j, q):
                    for i in range(n):
                        last = multiply(GROUP * q + a + i, (src[:, i, 0, :], src[:, i, 1, :]),
                                        acc_early[:, j * P:(j + 1) * P], acc_late[:, j * P:(j + 1) * P])
                if j == ROWS - 1:
                    last.then_inc(s_group, 1)

            def chunk0(c, first, final):
                for j in range(ROWS):
                    for q in range(GROUPS):
                        if q + 2 < GROUPS:
                            transpose_group(c, j, q + 2)
                        elif j + 1 < ROWS:
                            transpose_group(c, j + 1, q + 2 - GROUPS)
                        elif not final:
                            transpose_group(c + 1, 0, q + 2 - GROUPS)
                        if q == 0 and j == ROWS - 1:
                            pe.wait_ge(s_diag, ROWS * (c + 1))
                            if not first:
                                pe.wait_ge(s_h2, c)
                            for i in range(ROWS):
                                last = nc.tensor.matmul(m1[:, i * P:(i + 1) * P], ones[:, :], diag[:, i, :],
                                                        start=True, stop=True)
                            last.then_inc(s_bcast, 1)
                        multiply_group(c, j, q, first)
                    if not first:
                        step(0, c - 1, j)

            def chunk(s, c, before):
                n = everywhere(s, c) - 1
                for k in range(TILES):
                    q = k // GROUP
                    if k % GROUP == 0 and isinstance(c, int):
                        pe.wait_ge(s_xtail, GROUPS * s + q + 1)
                    if k == 0:
                        pe.wait_ge(s_early, n)
                    if k == LATE:
                        pe.wait_ge(s_zsum, n)
                    if k < RESIDENT:
                        parts = [home[:, c, :, k, i, :] for i in range(2)]
                    else:
                        g, i_k = divmod(k - RESIDENT, SLOT)
                        if i_k == 0:
                            pe.wait_ge(s_slot[g], (everywhere(s, c) - CHUNKS) * 16)
                        parts = [slot[g][:, :, i_k, i, :] for i in range(2)]
                    last = multiply(k, parts, tiles3(acc_early), tiles3(acc_late))
                    if k % GROUP == GROUP - 1:
                        last.then_inc(s_group, 1)
                        step(*before, q)

            pe.wait_ge(s_w, 16 * 5)
            pe.wait_ge(s_const, 1)
            pe.wait_ge(s_xtail, GROUPS)
            transpose_group(0, 0, 0)
            transpose_group(0, 0, 1)
            chunk0(0, True, False)
            with pe.Fori(1, CHUNKS - 1) as c:
                chunk0(c, False, False)
            chunk0(CHUNKS - 1, False, True)
            for s in range(1, LAST + 1):
                chunk(s, 0, (s - 1, CHUNKS - 1))
                with pe.Fori(1, CHUNKS) as c:
                    chunk(s, c, (s, c - 1))
            for k in range(3):
                step(LAST, CHUNKS - 1, k)


def kernel(**inputs):
    import concourse.bacc as bacc
    from concourse.bass_utils import run_bass_kernel_spmd as run

    a = {k: np.asarray(v) for k, v in inputs.items()}
    w = {f"{t}_W{i}": a[f"L0_gnn_{t}_W{i}"] for t in ("uv", "vu") for i in (1, 2, 3)}
    b = {f"{t}_b{i}": a[f"L0_gnn_{t}_b{i}"] for t in ("uv", "vu") for i in (1, 2, 3)}
    w.update(L1_WT=a["L1_gnn_W"].T, L2_WselfT=a["L2_gnn_W"][:, :FEAT].T, L2_WneighT=a["L2_gnn_W"][:, FEAT:].T,
             L3_W1=a["L3_gnn_W1"], L3_W2=a["L3_gnn_W2"])
    b.update(L1_b=a["L1_gnn_b"], L2_b=a["L2_gnn_b"])
    arrays = {
        "adj": np.ascontiguousarray(a["adj"]),
        "x": np.ascontiguousarray(a["x"]),
        "mats": np.stack([w[n] for n in MATS]),
        "cols": np.stack([b[n] for n in COLS], axis=1),
        "rowvecs": np.stack([b[n] for n in ROWVECS]),
        "filters": np.stack([np.ascontiguousarray(a[n].reshape(TILES, P).T) for n in ("L3_gnn_f1", "L3_gnn_f2")]),
        "alpha": np.ascontiguousarray(a["L1_gnn_alpha"].reshape(1, 1)),
    }
    nc = bacc.Bacc("TRN2", target_bir_lowering=False, num_devices=1)
    args = [nc.dram_tensor(n, v.shape, mybir.dt.from_np(v.dtype), kind="ExternalInput").ap() for n, v in arrays.items()]
    result = nc.dram_tensor("result", (NODES, FEAT), mybir.dt.float32, kind="ExternalOutput").ap()
    build(nc, *args, result)
    r = run(nc, [arrays], core_ids=[0])
    return r.results[0]["result"]
```

```python
import numpy as np
import concourse.bass as bass
from concourse import mybir
from contextlib import ExitStack

P = 128
NODES = 4096
FEAT = 128
TILES = NODES // P
CHUNK = 512
CHUNKS = NODES // CHUNK
ROWS = CHUNK // P
GROUP = 4
GROUPS = TILES // GROUP
LATE = TILES - GROUP
RESIDENT = 5
STREAMED = TILES - RESIDENT
SLOT = 3
SLOTS = STREAMED // SLOT
PAIR = 2 * P
PARTS = 4
PART = NODES // PARTS
PER_PART = GROUPS // PARTS
NAT = NODES * 2
ASM = STREAMED * PAIR
REGION = max(2 * NAT + NODES + ASM, SLOTS * ROWS * SLOT * PAIR)
TAILS_AFTER = (1, 3, 5, 7)
SCALES_AFTER = 2
LEAD = 2
PIECES = ((0, 1), (1, 3), (3, 6), (6, 9))
VECTOR_MOVES = (0, 1, 2, 3, 4, 5, 6, 7)
SCALAR_MOVES = tuple(q for q in range(GROUPS) if q not in VECTOR_MOVES)

EPS = 1e-5
SLOPE = 0.01
TOP = 14
SHRINK = NODES.bit_length() - 1
EXPONENT = 0x7F800000
MIRROR = float(254 << 23)
SMALLEST = 2.0 ** -111

STAGES = ["uv", "vu", "uv", "vu", "uv_norm", "conv1", "conv2", "filter1", "relu", "filter2", "out"]
LAST = len(STAGES) - 1
MLP = ("uv", "vu", "uv_norm")
CONV = ("conv1", "conv2")
NORM = ("uv_norm", "conv1", "conv2", "out")
MATS = ["uv_W1", "uv_W2", "uv_W3", "vu_W1", "vu_W2", "vu_W3", "L1_WT", "L2_WselfT", "L2_WneighT", "L3_W1", "L3_W2"]
COLS = ["uv_b1", "uv_b2", "vu_b1", "vu_b2"]
ROWVECS = ["uv_b3", "vu_b3", "L1_b", "L2_b"]


def nth(kinds, s, c):
    return CHUNKS * sum(STAGES[r] in kinds for r in range(s)) + c + 1


def everywhere(s, c):
    return CHUNKS * s + c + 1


def build(nc, adj, x, mats, cols, rowvecs, filters, alpha, out):
    f32, f16, bf16, i32 = mybir.dt.float32, mybir.dt.float16, mybir.dt.bfloat16, mybir.dt.int32
    ALU, ACT, AX = mybir.AluOpType, mybir.ActivationFunctionType, mybir.AxisListType
    AMAX = bass.bass_isa.ReduceOp.absmax

    adjT = nc.dram_tensor("adjT", (CHUNKS, SLOTS, P, ROWS * SLOT * PAIR), f16, kind="Internal").ap()
    x3_dram = nc.dram_tensor("x3", (TILES, P, FEAT), f32, kind="Internal").ap()
    adj_v = adj.rearrange("(t p) (h k) -> t h p k", p=P, h=PARTS)
    x_v = x.rearrange("(t p) f -> p t f", p=P)
    out_v = out.rearrange("(t p) f -> t p f", p=P)

    with ExitStack() as ctx:
        def sb(name, shape, dt):
            return ctx.enter_context(nc.sbuf_tensor(name, shape, dt))

        def bank(name):
            return ctx.enter_context(nc.psum_tensor(name, [P, CHUNK], f32))

        def sem(name):
            return ctx.enter_context(nc.semaphore(name))

        home = sb("home", [P, CHUNKS, ROWS, RESIDENT, 2, P], f16)
        region = sb("region", [P, REGION], f16)
        nat = [region[:, b * NAT:(b + 1) * NAT].bitcast(f32) for b in range(2)]
        nat_tail = [region[:, b * NAT:(b + 1) * NAT].rearrange("p (k two) -> p k two", two=2)[:, :, 0] for b in range(2)]
        nat_head = region[:, 2 * NAT:2 * NAT + NODES]
        asm = region[:, 2 * NAT + NODES:2 * NAT + NODES + ASM].rearrange("p (k h n) -> p k h n", h=2, n=P)
        slot_flat = [region[:, g * ROWS * SLOT * PAIR:(g + 1) * ROWS * SLOT * PAIR] for g in range(SLOTS)]
        slot = [v.rearrange("p (j k h n) -> p j k h n", k=SLOT, h=2, n=P) for v in slot_flat]
        x_parts = sb("x_parts", [P, TILES, 2, FEAT], f16)
        x_f32 = sb("x_f32", [P, TILES, FEAT], f32)
        x_rows = x_f32[:, :, :].rearrange("p t f -> p (t f)")
        undo_row = sb("undo_row", [P, CHUNKS, CHUNK], bf16)
        mat = sb("mat", [P, len(MATS), FEAT], f32)
        kept = sb("kept", [P, FEAT], f32)
        mixed = sb("mixed", [P, FEAT], f32)
        col = sb("col", [P, len(COLS)], f32)
        vec = sb("vec", [P, len(ROWVECS), FEAT], f32)
        filt = sb("filt", [P, 2, TILES], f32)
        alpha_c = sb("alpha_c", [P, 1], f32)
        beta_c = sb("beta_c", [P, 1], f32)
        eps_c = sb("eps_c", [P, 1], f32)
        ident = sb("ident", [P, P], f32)
        ident16 = sb("ident16", [P, P], f16)
        ones = sb("ones", [P, P], f32)
        diag = sb("diag", [P, ROWS, P], f32)
        part_mean = sb("part_mean", [P, PARTS], f32)
        magnitudes = sb("magnitudes", [P, PART], bf16)
        row_mean = sb("row_mean", [P, 1], f32)
        row_exp = sb("row_exp", [P, 1], f32)
        row_undo = sb("row_undo", [P, ROWS], f32)
        chunk_undo = sb("chunk_undo", [P, ROWS], f32)
        row_scale = sb("row_scale", [P, ROWS], f32)
        part_row_sum = sb("part_row_sum", [P, ROWS, PARTS], f32)
        row_sum = sb("row_sum", [P, ROWS], f32)
        degree = sb("degree", [P, TILES], f32)
        nonzero = sb("nonzero", [P, TILES], f32)
        inv_degree = sb("inv_degree", [P, TILES], f32)
        chunk_max = sb("chunk_max", [P, CHUNKS], f32)
        part_max = sb("part_max", [P, 1], f32)
        all_max = sb("all_max", [P, 1], f32)
        x_exp = sb("x_exp", [P, 1], f32)
        x_scale = sb("x_scale", [P, 2, 2], f32)
        x_undo = sb("x_undo", [P, 2, 2], f32)
        early = sb("early", [P, CHUNK], f32)
        z = sb("z", [P, CHUNK], f32)
        biased = sb("biased", [P, CHUNK], f32)
        h1 = sb("h1", [P, CHUNK], f32)
        h2 = sb("h2", [P, CHUNK], f32)
        x_now = h2[:, :].rearrange("p (j f) -> p j f", j=ROWS)
        y = sb("y", [P, ROWS, FEAT], f32)
        ysum = biased[:, :].rearrange("p (j f) -> p j f", j=ROWS)
        stats = sb("stats", [P, ROWS, 6], f32)
        apart = sb("apart", [P, ROWS], f32)
        twice_mean = sb("twice_mean", [P, ROWS], f32)
        mean = sb("mean", [P, ROWS], f32)
        within = sb("within", [P, ROWS], f32)
        between = sb("between", [P, ROWS], f32)
        spread = sb("spread", [P, ROWS], f32)
        std = sb("std", [P, ROWS], f32)
        rstd = sb("rstd", [P, ROWS], f32)

        acc_early, acc_late = bank("acc_early"), bank("acc_late")
        turned = [ctx.enter_context(nc.psum_tensor(f"turned{i}", [P, 2 * CHUNK], f16)) for i in range(4)]
        m0, m1 = bank("m0"), bank("m1")

        s_x = sem("x_loaded")
        s_w = sem("weights_loaded")
        s_const = sem("constants_ready")
        s_ident = sem("identity_zeroed")
        s_nat = [[sem(f"nat{b}{h}_loaded") for h in range(PARTS)] for b in range(2)]
        s_stored = [sem(f"piece{i}_stored") for i in range(len(PIECES))]
        s_slot = [sem(f"slot{g}_loaded") for g in range(SLOTS)]
        s_pmean = sem("part_mean_ready")
        s_rmean = sem("row_mean_ready")
        s_rexp = sem("row_exponent_ready")
        s_rundo = sem("row_undo_ready")
        s_rscale = sem("row_scale_ready")
        s_nhead = sem("part_heads_ready")
        s_ntail = sem("part_tails_ready")
        s_turned = sem("blocks_transposed")
        s_smoved = sem("group_moved_by_scalar")
        s_vmoved = sem("group_moved_by_vector")
        s_diag = sem("diagonal_ready")
        s_bcast = sem("row_undo_broadcast")
        s_undo = sem("undo_row_ready")
        s_kept = sem("chunk_undo_kept")
        s_rsum = sem("row_sum_ready")
        s_deg = sem("degree_ready")
        s_setup = sem("setup_step")
        s_group = sem("group_multiplied")
        s_early = sem("early_read")
        s_zsum = sem("late_read")
        s_z = sem("z_ready")
        s_mm1 = sem("layer1_multiplied")
        s_biased1 = sem("layer1_biased")
        s_h1 = sem("h1_ready")
        s_mm2 = sem("layer2_multiplied")
        s_biased2 = sem("layer2_biased")
        s_h2 = sem("h2_ready")
        s_xnow = sem("x_now_copied")
        s_xt = sem("x_transposed")
        s_xtc = sem("x_transposed_copied")
        s_lin = sem("linear_done")
        s_linread = sem("linear_read")
        s_y = sem("y_ready")
        s_ysum = sem("y_sum_ready")
        s_stats = sem("stats_ready")
        s_apart = sem("apart_ready")
        s_within = sem("within_ready")
        s_between = sem("between_ready")
        s_mv = sem("mean_and_spread_ready")
        s_std = sem("std_ready")
        s_rstd = sem("rstd_ready")
        s_new = sem("new_x_ready")
        s_cmax = sem("chunk_max_ready")
        s_pmax = sem("partition_max_ready")
        s_amax = sem("all_max_ready")
        s_xexp = sem("x_exponent_ready")
        s_xundo = sem("x_undo_ready")
        s_xscale = sem("x_scale_ready")
        s_xhead = sem("x_head_ready")
        s_xtail = sem("x_parts_ready")
        s_reload = sem("residual_reloaded")
        s_spill = sem("x3_spilled")
        s_out = sem("out_stored")

        block = ctx.enter_context(nc.Block())

        def m(name):
            return mat[:, MATS.index(name), :]

        def column(name):
            return col[:, COLS.index(name):COLS.index(name) + 1]

        def per_row(name):
            return vec[:, ROWVECS.index(name), :].unsqueeze(1).to_broadcast([P, ROWS, FEAT])

        def rows(c):
            return slice(c * ROWS, (c + 1) * ROWS) if isinstance(c, int) else bass.ds(c * ROWS, ROWS)

        def following(c, j, n):
            return c + (j + n) // ROWS, (j + n) % ROWS

        def tiles3(psum):
            return psum[:, :].rearrange("p (j n) -> p j n", j=ROWS)

        def places(c, j, q):
            k0, k1 = GROUP * q, GROUP * (q + 1)
            if k0 < RESIDENT:
                n = min(k1, RESIDENT) - k0
                yield 0, n, home[:, c, j, k0:k0 + n, :, :]
            if k1 > RESIDENT:
                a = max(k0, RESIDENT)
                yield a - k0, k1 - a, asm[:, a - RESIDENT:k1 - RESIDENT, :, :]

        def moved(t, q):
            for done, groups in ((s_vmoved, VECTOR_MOVES), (s_smoved, SCALAR_MOVES)):
                if q in groups:
                    return done, t * len(groups) + groups.index(q) + 1

        def wait_moved(eng, t, q):
            eng.wait_ge(*moved(t, q))

        def move(eng, copy, c, j, q, moved):
            t = c * ROWS + j
            eng.wait_ge(s_turned, GROUPS * t + q + 1)
            if not (isinstance(t, int) and t == 0):
                blocks = range(max(GROUP * q, RESIDENT) - RESIDENT, GROUP * (q + 1) - RESIDENT)
                for i, (a, b) in enumerate(PIECES):
                    if set(blocks) & set(range(a * SLOT, b * SLOT)):
                        eng.wait_ge(s_stored[i], 16 * t)
            for a, n, dest in places(c, j, q):
                last = copy(dest.rearrange("p k h n -> p (k h n)"), turned[q % 4][:, a * PAIR:(a + n) * PAIR])
            last.then_inc(moved, 1)

        def x_count(s, late):
            return 1 if s == 0 else 2 * s + late

        def scale_at(table, s, late):
            late = late if s else 0
            return table[:, s % 2, late:late + 1]

        @block.sync
        def _(sp):
            def part(b, h):
                return nat[b][:, h * PART:(h + 1) * PART]

            for h in range(PARTS):
                sp.dma_start(part(0, h), adj_v[0, h]).then_inc(s_nat[0][h], 16)
            sp.dma_start(x_f32[:, :, :], x_v).then_inc(s_x, 16)
            for h in range(PARTS):
                sp.dma_start(part(1, h), adj_v[1, h]).then_inc(s_nat[1][h], 16)

            def load(c, j, h):
                sp.wait_ge(s_turned, GROUPS * (c * ROWS + j) + PER_PART * (h + 1))
                sp.dma_start(part(j % 2, h), adj_v[c * ROWS + j + 2, h]).then_inc(s_nat[j % 2][h], 16)

            def store(c, j, i):
                wait_moved(sp, c * ROWS + j, 2 * i + 1)
                a, b = PIECES[i]
                sp.dma_start(
                    adjT[c, a:b, :, j * SLOT * PAIR:(j + 1) * SLOT * PAIR].rearrange("g p e -> p g e"),
                    asm[:, a * SLOT:b * SLOT, :, :].rearrange("p (g k) h n -> p g (k h n)", k=SLOT),
                ).then_inc(s_stored[i], 16)

            def row_tile(c, j, more):
                for h in range(PARTS):
                    if more:
                        load(c, j, h)
                    if h:
                        store(c, j, h - 1)
                store(c, j, PARTS - 1)

            with sp.Fori(0, CHUNKS - 1) as c:
                for j in range(ROWS):
                    row_tile(c, j, True)
            for j in range(ROWS):
                row_tile(CHUNKS - 1, j, j + 2 < ROWS)
            sp.wait_ge(s_group, GROUPS * CHUNKS)
            for stored in s_stored:
                sp.wait_ge(stored, 16 * TILES)
            with sp.Fori(1, LAST + 1) as s:
                with sp.Fori(0, CHUNKS) as c:
                    for g in range(SLOTS):
                        last_group = (RESIDENT + SLOT * (g + 1) - 1) // GROUP
                        sp.wait_ge(s_group, s * (GROUPS * CHUNKS) + c * GROUPS - GROUPS + last_group + 1)
                        sp.dma_start(slot_flat[g], adjT[c, g]).then_inc(s_slot[g], 16)

        @block.gpsimd
        def _(pool):
            nc.gpsimd.memset(ident[:, :], 0.0).then_inc(s_ident, 1)
            nc.gpsimd.memset(ones[:, :], 1.0)
            nc.gpsimd.memset(eps_c[:, :], EPS)
            pool.wait_ge(s_ident, 1)
            nc.gpsimd.affine_select(out=ident[:, :], in_=ident[:, :], compare_op=ALU.not_equal, fill=1.0, base=0,
                                    pattern=[[-1, P]], channel_multiplier=1).then_inc(s_const, 1)
            pool.wait_ge(s_const, 1)
            nc.gpsimd.tensor_copy(ident16[:, :], ident[:, :]).then_inc(s_const, 1)

            def reduce_max(s, late):
                pool.wait_ge(s_pmax, x_count(s, late))
                nc.gpsimd.partition_all_reduce(all_max[:, :], part_max[:, :], P, AMAX).then_inc(s_amax, 1)

            def reload(s, source):
                for c in range(CHUNKS):
                    pool.wait_ge(s_xtail, CHUNKS * s + c + 1)
                    pool.dma_start(x_f32[:, c * ROWS:(c + 1) * ROWS, :],
                                   source[:, c * ROWS:(c + 1) * ROWS, :]).then_inc(s_reload, 16)

            def write_rows(s, c, dest, done):
                pool.wait_ge(s_new, everywhere(s, c))
                pool.dma_start(dest[rows(c), :, :].rearrange("t p f -> p t f"), x_f32[:, rows(c), :]).then_inc(done, 16)

            reduce_max(0, 0)
            for s in range(LAST + 1):
                if STAGES[s] == "uv_norm":
                    reload(s, x_v)
                if STAGES[s] == "out":
                    pool.wait_ge(s_spill, 16 * CHUNKS)
                    reload(s, x3_dram.rearrange("t p f -> p t f"))
                for c in range(CHUNKS):
                    if STAGES[s] == "conv2":
                        write_rows(s, c, x3_dram, s_spill)
                    if STAGES[s] == "out":
                        write_rows(s, c, out_v, s_out)
                    if s < LAST and c >= CHUNKS - 2:
                        reduce_max(s + 1, int(c == CHUNKS - 1))
            pool.wait_ge(s_out, 16 * CHUNKS)

        @block.scalar
        def _(act):
            act.dma_start(mat[:, :, :], mats.rearrange("m p f -> p m f")).then_inc(s_w, 16)
            act.dma_start(col[:, :], cols).then_inc(s_w, 16)
            act.dma_start(vec[:, :, :], rowvecs.unsqueeze(0).to_broadcast([P, len(ROWVECS), FEAT])).then_inc(s_w, 16)
            act.dma_start(filt[:, :, :], filters.rearrange("a p t -> p a t")).then_inc(s_w, 16)
            act.dma_start(alpha_c[:, :], alpha.to_broadcast([P, 1])).then_inc(s_w, 16)

            def row_magnitudes(c, j, h):
                t = c * ROWS + j
                act.wait_ge(s_nat[j % 2][h], 16 * (c * (ROWS // 2) + j // 2 + 1))
                if h == 0 and not (isinstance(t, int) and t == 0):
                    act.wait_ge(s_rmean, t)
                if h or not (isinstance(t, int) and t == 0):
                    act.wait_ge(s_pmean, PARTS * t + h)
                nc.scalar.activation(magnitudes[:, :], nat[j % 2][:, h * PART:(h + 1) * PART], ACT.Abs,
                                     scale=2.0 ** -SHRINK, accum_out=part_mean[:, h:h + 1]).then_inc(s_pmean, 1)

            def nat_heads(c, j, h):
                t = c * ROWS + j
                act.wait_ge(s_rscale, t + 1)
                if not (isinstance(t, int) and t == 0):
                    act.wait_ge(s_turned, GROUPS * (t - 1) + PER_PART * (h + 1))
                if j == 0 and h == 0 and not (isinstance(t, int) and t == 0):
                    act.wait_ge(s_rsum, c)
                nc.scalar.activation(nat_head[:, h * PART:(h + 1) * PART], nat[j % 2][:, h * PART:(h + 1) * PART],
                                     ACT.Copy, scale=row_scale[:, j:j + 1],
                                     accum_out=part_row_sum[:, j, h:h + 1]).then_inc(s_nhead, 1)

            def copy(dest, src):
                return nc.scalar.activation(dest, src, ACT.Copy)

            def read_early(s, c):
                act.wait_ge(s_group, GROUPS * everywhere(s, c) - 1)
                if s or not (isinstance(c, int) and c == 0):
                    act.wait_ge(s_zsum, everywhere(s, c) - 1)
                nc.scalar.activation(early[:, :], acc_early[:, :], ACT.Copy,
                                     scale=scale_at(x_undo, s, 0)).then_inc(s_early, 1)

            def hidden1(s, c):
                act.wait_ge(s_mm1, nth(MLP, s, c))
                nc.scalar.activation(biased[:, :], m0[:, :], ACT.Identity,
                                     bias=column(STAGES[s][:2] + "_b1")).then_inc(s_biased1, 1)

            def hidden2(s, c):
                act.wait_ge(s_mm2, nth(MLP, s, c))
                nc.scalar.activation(biased[:, :], m1[:, :], ACT.Identity,
                                     bias=column(STAGES[s][:2] + "_b2")).then_inc(s_biased2, 1)

            def after(s, c):
                if STAGES[s] in MLP:
                    hidden1(s, c)
                    hidden2(s, c)
                if STAGES[s] in CONV:
                    act.wait_ge(s_lin, everywhere(s, c) - 1)
                    nc.scalar.activation(x_now[:, :, :], x_f32[:, rows(c), :], ACT.Copy).then_inc(s_xnow, 1)
                    act.wait_ge(s_xt, nth(CONV, s, c))
                    nc.scalar.activation(h1[:, :], m1[:, :], ACT.Copy).then_inc(s_xtc, 1)
                if STAGES[s] in NORM:
                    act.wait_ge(s_mv, nth(NORM, s, c))
                    nc.scalar.activation(std[:, :], spread[:, :], ACT.Sqrt, bias=eps_c[:, 0:1],
                                     scale=1.0 / FEAT).then_inc(s_std, 1)

            def x_head(s, b):
                act.wait_ge(s_xscale, x_count(s, int(b == GROUPS - 1)))
                if s:
                    act.wait_ge(s_group, GROUPS * CHUNKS * s - GROUPS + b + 1)
                nc.scalar.activation(x_parts[:, b * GROUP:(b + 1) * GROUP, 0, :], x_f32[:, b * GROUP:(b + 1) * GROUP, :],
                                     ACT.Copy, scale=scale_at(x_scale, s, int(b == GROUPS - 1))).then_inc(s_xhead, 1)

            act.wait_ge(s_w, 16 * 5)
            act.wait_ge(s_const, 1)
            for h in range(PARTS):
                row_magnitudes(0, 0, h)
            for h in range(PARTS - 1):
                nat_heads(0, 0, h)
                row_magnitudes(0, 1, h)
            for b in range(GROUPS):
                x_head(0, b)

            def chunk0(c, first, final):
                for j in range(ROWS):
                    t1, t2 = following(c, j, 1), following(c, j, 2)
                    left = ROWS - 1 - j if final else ROWS
                    for q in range(GROUPS):
                        if q % PER_PART == 0:
                            h = q // PER_PART - 1
                            if h < 0:
                                if left >= 1:
                                    row_magnitudes(*t1, PARTS - 1)
                                nat_heads(c, j, PARTS - 1)
                            else:
                                if left >= 1:
                                    nat_heads(*t1, h)
                                if left >= 2:
                                    row_magnitudes(*t2, h)
                        if q in SCALAR_MOVES:
                            move(act, copy, c, j, q, s_smoved)
                        if q == 1 and j == 0 and not first:
                            read_early(0, c - 1)
                        if q == 1 and j == 1 and not first:
                            hidden1(0, c - 1)
                        if q == 1 and j == 2 and not first:
                            hidden2(0, c - 1)

            chunk0(0, True, False)
            with act.Fori(1, CHUNKS - 1) as c:
                chunk0(c, False, False)
            chunk0(CHUNKS - 1, False, True)
            for b in range(GROUPS - 1):
                x_head(1, b)
            read_early(0, CHUNKS - 1)
            after(0, CHUNKS - 1)
            x_head(1, GROUPS - 1)

            for s in range(1, LAST + 1):
                with act.Fori(0, CHUNKS - 1) as c:
                    read_early(s, c)
                    after(s, c)
                if s < LAST:
                    for b in range(GROUPS - 1):
                        x_head(s + 1, b)
                read_early(s, CHUNKS - 1)
                after(s, CHUNKS - 1)
                if s < LAST:
                    x_head(s + 1, GROUPS - 1)

        @block.vector
        def _(dve):
            def power_of_two(largest, top, exponent, undo, scale, s_exp, s_und, s_sc, n):
                nc.vector.tensor_scalar(exponent.bitcast(i32), largest.bitcast(i32), EXPONENT, None,
                                        ALU.bitwise_and).then_inc(s_exp, 1)
                dve.wait_ge(s_exp, n)
                nc.vector.tensor_scalar(undo, exponent, SMALLEST, 2.0 ** -top, ALU.max, ALU.mult).then_inc(s_und, 1)
                dve.wait_ge(s_und, n)
                nc.vector.tensor_scalar(scale.bitcast(i32), undo.bitcast(i32), -1.0, MIRROR,
                                        ALU.mult, ALU.add).then_inc(s_sc, 1)

            def row_scales(c, j, first):
                t = c * ROWS + j
                dve.wait_ge(s_pmean, PARTS * (t + 1))
                nc.vector.tensor_reduce(row_mean[:, :], part_mean[:, :], axis=AX.X, op=ALU.add).then_inc(s_rmean, 1)
                dve.wait_ge(s_rmean, t + 1)
                power_of_two(row_mean[:, :], TOP - SHRINK, row_exp[:, :], row_undo[:, j:j + 1], row_scale[:, j:j + 1],
                             s_rexp, s_rundo, s_rscale, t + 1)
                if j == 0 and not first:
                    dve.wait_ge(s_bcast, c)
                nc.vector.tensor_scalar(diag[:, j, :], ident[:, :], row_undo[:, j:j + 1], None,
                                        ALU.mult).then_inc(s_diag, 1)

            def nat_tails(c, j, h):
                dve.wait_ge(s_nhead, PARTS * (c * ROWS + j) + h + 1)
                nc.vector.scalar_tensor_tensor(nat_tail[j % 2][:, h * PART:(h + 1) * PART],
                                               nat[j % 2][:, h * PART:(h + 1) * PART], row_scale[:, j:j + 1],
                                               nat_head[:, h * PART:(h + 1) * PART],
                                               ALU.mult, ALU.subtract).then_inc(s_ntail, 1)

            def sum_products(s, c):
                n = everywhere(s, c)
                dve.wait_ge(s_group, GROUPS * n)
                dve.wait_ge(s_early, n)
                nc.vector.scalar_tensor_tensor(z[:, :], acc_late[:, :], scale_at(x_undo, s, 1), early[:, :],
                                               ALU.mult, ALU.add).then_inc(s_zsum, 1)
                dve.wait_ge(s_zsum, n)
                if s or not (isinstance(c, int) and c == 0):
                    dve.wait_ge(s_lin, n - 1)
                nc.vector.tensor_tensor(z[:, :], z[:, :], undo_row[:, c, :], ALU.mult).then_inc(s_z, 1)

            def leaky(s, c, s_biased, h, s_h):
                dve.wait_ge(s_biased, nth(MLP, s, c))
                nc.vector.scalar_tensor_tensor(h[:, :], biased[:, :], SLOPE, biased[:, :],
                                               ALU.mult, ALU.max).then_inc(s_h, 1)

            def hidden(s, c):
                if STAGES[s] in MLP:
                    leaky(s, c, s_biased1, h1, s_h1)
                    leaky(s, c, s_biased2, h2, s_h2)

            def finish(s, c):
                kind = STAGES[s]
                n = everywhere(s, c)
                x_c = x_f32[:, rows(c), :]
                lin = tiles3(m0)
                dve.wait_ge(s_lin, n)
                if kind == "filter1":
                    dve.wait_ge(s_spill, 16 * CHUNKS)
                if kind in ("uv_norm", "out"):
                    dve.wait_ge(s_reload, 16 * CHUNKS * (1 + (kind == "out")))
                if kind in MLP:
                    nc.vector.tensor_tensor(y[:, :, :], lin, per_row(kind[:2] + "_b3"), ALU.add).then_inc(s_linread, 1)
                    dve.wait_ge(s_linread, n)
                    if kind == "uv_norm":
                        nc.vector.scalar_tensor_tensor(ysum[:, :, :], y[:, :, :], SLOPE, y[:, :, :],
                                                       ALU.mult, ALU.max).then_inc(s_y, 1)
                        dve.wait_ge(s_y, nth(("uv_norm", "conv1"), s, c))
                        nc.vector.tensor_tensor(y[:, :, :], ysum[:, :, :], x_c, ALU.add).then_inc(s_ysum, 1)
                    else:
                        nc.vector.scalar_tensor_tensor(x_c, y[:, :, :], SLOPE, y[:, :, :],
                                                       ALU.mult, ALU.max).then_inc(s_new, 1)
                elif kind == "conv1":
                    inv = inv_degree[:, rows(c)].unsqueeze(2).to_broadcast([P, ROWS, FEAT])
                    nc.vector.tensor_tensor(ysum[:, :, :], lin, inv, ALU.mult).then_inc(s_linread, 1)
                    dve.wait_ge(s_linread, n)
                    nc.vector.tensor_tensor(ysum[:, :, :], ysum[:, :, :], per_row("L1_b"), ALU.add).then_inc(s_y, 1)
                    dve.wait_ge(s_y, nth(("uv_norm", "conv1"), s, c))
                    nc.vector.scalar_tensor_tensor(y[:, :, :], ysum[:, :, :], 0.0, x_c,
                                                   ALU.max, ALU.add).then_inc(s_ysum, 1)
                elif kind == "conv2":
                    nc.vector.tensor_tensor(ysum[:, :, :], lin, per_row("L2_b"), ALU.add).then_inc(s_linread, 1)
                    dve.wait_ge(s_linread, n)
                    nc.vector.tensor_tensor(y[:, :, :], ysum[:, :, :], x_c, ALU.add).then_inc(s_ysum, 1)
                elif kind in ("filter1", "filter2"):
                    f = filt[:, int(kind == "filter2"), rows(c)].unsqueeze(2).to_broadcast([P, ROWS, FEAT])
                    nc.vector.tensor_tensor(x_c, lin, f, ALU.mult).then_inc(s_new, 1)
                elif kind == "relu":
                    nc.vector.tensor_scalar(x_c, lin, 0.0, None, ALU.max).then_inc(s_new, 1)
                else:
                    nc.vector.tensor_tensor(y[:, :, :], lin, x_c, ALU.add).then_inc(s_ysum, 1)
                if kind in NORM:
                    k = nth(NORM, s, c)
                    dve.wait_ge(s_ysum, k)
                    for j in range(ROWS):
                        last = nc.vector.bn_stats(stats[:, j, :], y[:, j, :])
                    last.then_inc(s_stats, 1)
                    dve.wait_ge(s_stats, k)
                    nc.vector.tensor_tensor(apart[:, :], stats[:, :, 1], stats[:, :, 4], ALU.subtract).then_inc(s_apart, 1)
                    nc.vector.tensor_tensor(twice_mean[:, :], stats[:, :, 1], stats[:, :, 4], ALU.add)
                    nc.vector.tensor_tensor(within[:, :], stats[:, :, 2], stats[:, :, 5], ALU.add).then_inc(s_within, 1)
                    dve.wait_ge(s_apart, k)
                    nc.vector.scalar_tensor_tensor(between[:, :], apart[:, :], FEAT / 4.0, apart[:, :],
                                                   ALU.mult, ALU.mult).then_inc(s_between, 1)
                    dve.wait_ge(s_within, k)
                    nc.vector.tensor_scalar(mean[:, :], twice_mean[:, :], 0.5, None, ALU.mult)
                    dve.wait_ge(s_between, k)
                    nc.vector.tensor_tensor(spread[:, :], within[:, :], between[:, :], ALU.add).then_inc(s_mv, 1)
                    dve.wait_ge(s_std, k)
                    nc.vector.reciprocal(rstd[:, :], std[:, :]).then_inc(s_rstd, 1)
                    dve.wait_ge(s_rstd, k)
                    for j in range(ROWS):
                        x_j = x_f32[:, c * ROWS + j, :]
                        last = nc.vector.tensor_scalar(x_j, y[:, j, :], mean[:, j:j + 1], rstd[:, j:j + 1],
                                                       ALU.subtract, ALU.mult)
                    last.then_inc(s_new, 1)
                if s < LAST:
                    dve.wait_ge(s_new, n)
                    nc.vector.tensor_reduce(chunk_max[:, bass.ds(c, 1)] if not isinstance(c, int) else
                                            chunk_max[:, c:c + 1], x_c, axis=AX.XY, op=ALU.max,
                                            apply_absolute_value=True).then_inc(s_cmax, 1)

            def x_largest():
                nc.vector.tensor_reduce(part_max[:, :], x_rows, axis=AX.X, op=ALU.max,
                                        apply_absolute_value=True).then_inc(s_pmax, 1)

            def x_scales(s, late):
                n = x_count(s, late)
                if s:
                    dve.wait_ge(s_cmax, everywhere(s - 1, CHUNKS - 1 if late else CHUNKS - 2))
                    src = chunk_max[:, CHUNKS - 1:CHUNKS] if late else chunk_max[:, 0:CHUNKS - 1]
                    nc.vector.tensor_reduce(part_max[:, :], src, axis=AX.X, op=ALU.max).then_inc(s_pmax, 1)
                dve.wait_ge(s_amax, n)
                at = late if s else 0
                power_of_two(all_max[:, :], TOP, x_exp[:, :], x_undo[:, s % 2, at:at + 1], x_scale[:, s % 2, at:at + 1],
                             s_xexp, s_xundo, s_xscale, n)
                dve.wait_ge(s_xscale, n)

            def x_tail(s, b):
                dve.wait_ge(s_xhead, GROUPS * s + b + 1)
                nc.vector.scalar_tensor_tensor(x_parts[:, b * GROUP:(b + 1) * GROUP, 1, :],
                                               x_f32[:, b * GROUP:(b + 1) * GROUP, :],
                                               scale_at(x_scale, s, int(b == GROUPS - 1)),
                                               x_parts[:, b * GROUP:(b + 1) * GROUP, 0, :],
                                               ALU.mult, ALU.subtract).then_inc(s_xtail, 1)

            dve.wait_ge(s_const, 1)
            row_scales(0, 0, True)
            dve.wait_ge(s_x, 16)
            x_largest()
            nat_tails(0, 0, 0)
            nat_tails(0, 0, 1)
            x_scales(0, 0)
            for b in range(GROUPS):
                x_tail(0, b)

            def chunk0(c, first, final):
                for j in range(ROWS):
                    nxt = (c + (j + 1) // ROWS, (j + 1) % ROWS)
                    ahead = not (final and j == ROWS - 1)
                    for q in range(GROUPS):
                        if q in VECTOR_MOVES:
                            move(dve, nc.vector.tensor_copy, c, j, q, s_vmoved)
                        if q in TAILS_AFTER:
                            h = TAILS_AFTER.index(q) + 2
                            if h < PARTS:
                                nat_tails(c, j, h)
                            elif ahead:
                                nat_tails(*nxt, h - PARTS)
                        if q == 1 and j == ROWS - 1:
                            dve.wait_ge(s_bcast, c + 1)
                            nc.vector.tensor_copy(undo_row[:, c, :], m1[:, :]).then_inc(s_undo, 1)
                            nc.vector.tensor_copy(chunk_undo[:, :], row_undo[:, :]).then_inc(s_kept, 1)
                            dve.wait_ge(s_kept, c + 1)
                        if q == SCALES_AFTER and ahead:
                            row_scales(*nxt, False)
                        if q == SCALES_AFTER and j == ROWS - 1:
                            dve.wait_ge(s_nhead, PARTS * ROWS * (c + 1))
                            nc.vector.tensor_reduce(row_sum[:, :], part_row_sum[:, :, :], axis=AX.X,
                                                    op=ALU.add).then_inc(s_rsum, 1)
                            dve.wait_ge(s_rsum, c + 1)
                            nc.vector.tensor_tensor(degree[:, rows(c)], row_sum[:, :], chunk_undo[:, :],
                                                    ALU.mult).then_inc(s_deg, 1)
                            dve.wait_ge(s_deg, c + 1)
                        if q == 0 and j == 0 and not first:
                            dve.wait_ge(s_undo, c)
                            sum_products(0, c - 1)
                        if q == 4 and j == 1 and not first:
                            leaky(0, c - 1, s_biased1, h1, s_h1)
                        if q == 4 and j == 2 and not first:
                            leaky(0, c - 1, s_biased2, h2, s_h2)
                        if q == 6 and j == 3 and not first:
                            finish(0, c - 1)

            chunk0(0, True, False)
            with dve.Fori(1, CHUNKS - 1) as c:
                chunk0(c, False, False)
            chunk0(CHUNKS - 1, False, True)
            x_scales(1, 0)
            for b in range(GROUPS - 1):
                x_tail(1, b)
            dve.wait_ge(s_undo, CHUNKS)
            sum_products(0, CHUNKS - 1)
            hidden(0, CHUNKS - 1)
            finish(0, CHUNKS - 1)
            x_scales(1, 1)
            x_tail(1, GROUPS - 1)

            steps = [0]

            def setup(instruction):
                steps[0] += 1
                instruction.then_inc(s_setup, 1)
                dve.wait_ge(s_setup, steps[0])

            dve.wait_ge(s_w, 16 * 5)
            dve.wait_ge(s_deg, CHUNKS)
            setup(nc.vector.tensor_scalar(beta_c[:, :], alpha_c[:, :], -1.0, 1.0, ALU.mult, ALU.add))
            setup(nc.vector.tensor_scalar(mixed[:, :], m("L1_WT"), alpha_c[:, 0:1], None, ALU.mult))
            setup(nc.vector.tensor_scalar(kept[:, :], m("L1_WT"), beta_c[:, 0:1], None, ALU.mult))
            setup(nc.vector.tensor_scalar(degree[:, :], degree[:, :], alpha_c[:, 0:1], beta_c[:, 0:1],
                                          ALU.mult, ALU.add))
            setup(nc.vector.tensor_scalar(nonzero[:, :], degree[:, :], 0.0, None, ALU.is_equal))
            setup(nc.vector.tensor_tensor(degree[:, :], degree[:, :], nonzero[:, :], ALU.add))
            setup(nc.vector.tensor_scalar(nonzero[:, :], nonzero[:, :], -1.0, 1.0, ALU.mult, ALU.add))
            setup(nc.vector.reciprocal(inv_degree[:, :], degree[:, :]))
            setup(nc.vector.tensor_tensor(inv_degree[:, :], inv_degree[:, :], nonzero[:, :], ALU.mult))

            for s in range(1, LAST + 1):
                with dve.Fori(0, CHUNKS - 1) as c:
                    sum_products(s, c)
                    hidden(s, c)
                    finish(s, c)
                if s < LAST:
                    x_scales(s + 1, 0)
                    for b in range(GROUPS - 1):
                        x_tail(s + 1, b)
                sum_products(s, CHUNKS - 1)
                hidden(s, CHUNKS - 1)
                finish(s, CHUNKS - 1)
                if s < LAST:
                    x_scales(s + 1, 1)
                    x_tail(s + 1, GROUPS - 1)

        @block.tensor
        def _(pe):
            def multiply(k, head_and_tail, early_to, late_to):
                to = early_to if k < LATE else late_to
                head, tail = head_and_tail
                first, last = k in (0, LATE), k in (LATE - 1, TILES - 1)
                nc.tensor.matmul(to, x_parts[:, k, 0, :], head, start=first, stop=False)
                nc.tensor.matmul(to, x_parts[:, k, 0, :], tail, start=False, stop=False)
                return nc.tensor.matmul(to, x_parts[:, k, 1, :], head, start=False, stop=last)

            def free_m0(s, c):
                if s or not (isinstance(c, int) and c == 0):
                    pe.wait_ge(s_new, everywhere(s, c) - 1)

            def step(s, c, k):
                kind = STAGES[s]
                if kind in MLP:
                    w = kind[:2]
                    if k == 0:
                        pe.wait_ge(s_z, everywhere(s, c))
                        free_m0(s, c)
                        nc.tensor.matmul(m0[:, :], m(w + "_W1"), z[:, :], start=True, stop=True).then_inc(s_mm1, 1)
                    if k == 1:
                        pe.wait_ge(s_h1, nth(MLP, s, c))
                        if s == 0:
                            pe.wait_ge(s_undo, c + 1)
                        nc.tensor.matmul(m1[:, :], m(w + "_W2"), h1[:, :], start=True, stop=True).then_inc(s_mm2, 1)
                    if k == 2:
                        pe.wait_ge(s_h2, nth(MLP, s, c))
                        for j in range(ROWS):
                            last = nc.tensor.matmul(m0[:, j * P:(j + 1) * P], h2[:, j * P:(j + 1) * P], m(w + "_W3"),
                                                    start=True, stop=True)
                        last.then_inc(s_lin, 1)
                    return
                if kind in CONV:
                    if k == 0:
                        pe.wait_ge(s_xnow, nth(CONV, s, c))
                        for j in range(ROWS):
                            last = nc.tensor.transpose(m1[:, j * P:(j + 1) * P], x_now[:, j, :], ident[:, :])
                        last.then_inc(s_xt, 1)
                    if k == 1:
                        own, neigh = (kept[:, :], mixed[:, :]) if kind == "conv1" else (m("L2_WselfT"), m("L2_WneighT"))
                        pe.wait_ge(s_z, everywhere(s, c))
                        pe.wait_ge(s_xtc, nth(CONV, s, c))
                        free_m0(s, c)
                        for j in range(ROWS):
                            nc.tensor.matmul(m0[:, j * P:(j + 1) * P], z[:, j * P:(j + 1) * P], neigh,
                                             start=True, stop=False)
                            last = nc.tensor.matmul(m0[:, j * P:(j + 1) * P], h1[:, j * P:(j + 1) * P], own,
                                                    start=False, stop=True)
                        last.then_inc(s_lin, 1)
                    return
                if k == 0:
                    pe.wait_ge(s_z, everywhere(s, c))
                    free_m0(s, c)
                    for j in range(ROWS):
                        z_j, to = z[:, j * P:(j + 1) * P], m0[:, j * P:(j + 1) * P]
                        if kind in ("relu", "out"):
                            last = nc.tensor.transpose(to, z_j, ident[:, :])
                        else:
                            last = nc.tensor.matmul(to, z_j, m("L3_W1" if kind == "filter1" else "L3_W2"),
                                                    start=True, stop=True)
                    last.then_inc(s_lin, 1)

            def transpose_group(c, j, q):
                t, h = c * ROWS + j, q // PER_PART
                pe.wait_ge(s_ntail, PARTS * t + h + 1)
                if q >= 4:
                    wait_moved(pe, t, q - 4)
                elif not (isinstance(t, int) and t == 0):
                    wait_moved(pe, t - 1, q + 4)
                for i in range(GROUP):
                    at = slice((GROUP * q + i) * P, (GROUP * q + i + 1) * P)
                    nc.tensor.transpose(turned[q % 4][:, i * PAIR:i * PAIR + P], nat_head[:, at], ident16[:, :])
                    last = nc.tensor.transpose(turned[q % 4][:, i * PAIR + P:(i + 1) * PAIR],
                                               nat_tail[j % 2][:, at], ident16[:, :])
                last.then_inc(s_turned, 1)

            def multiply_group(c, j, q, first):
                wait_moved(pe, c * ROWS + j, q)
                if j == 0 and q == 0 and not first:
                    pe.wait_ge(s_early, c)
                if j == 0 and q == GROUPS - 1 and not first:
                    pe.wait_ge(s_zsum, c)
                for a, n, src in places(c, j, q):
                    for i in range(n):
                        last = multiply(GROUP * q + a + i, (src[:, i, 0, :], src[:, i, 1, :]),
                                        acc_early[:, j * P:(j + 1) * P], acc_late[:, j * P:(j + 1) * P])
                if j == ROWS - 1:
                    last.then_inc(s_group, 1)

            def chunk0(c, first, final):
                for j in range(ROWS):
                    for q in range(GROUPS):
                        if q + LEAD < GROUPS:
                            transpose_group(c, j, q + LEAD)
                        elif j + 1 < ROWS:
                            transpose_group(c, j + 1, q + LEAD - GROUPS)
                        elif not final:
                            transpose_group(c + 1, 0, q + LEAD - GROUPS)
                        if q == 0 and j == ROWS - 1:
                            pe.wait_ge(s_diag, ROWS * (c + 1))
                            if not first:
                                pe.wait_ge(s_h2, c)
                            for i in range(ROWS):
                                last = nc.tensor.matmul(m1[:, i * P:(i + 1) * P], ones[:, :], diag[:, i, :],
                                                        start=True, stop=True)
                            last.then_inc(s_bcast, 1)
                        multiply_group(c, j, q, first)
                    if not first:
                        step(0, c - 1, j)

            def chunk(s, c, before):
                n = everywhere(s, c) - 1
                for k in range(TILES):
                    q = k // GROUP
                    if k % GROUP == 0 and isinstance(c, int):
                        pe.wait_ge(s_xtail, GROUPS * s + q + 1)
                    if k == 0:
                        pe.wait_ge(s_early, n)
                    if k == LATE:
                        pe.wait_ge(s_zsum, n)
                    if k < RESIDENT:
                        parts = [home[:, c, :, k, i, :] for i in range(2)]
                    else:
                        g, i_k = divmod(k - RESIDENT, SLOT)
                        if i_k == 0:
                            pe.wait_ge(s_slot[g], (everywhere(s, c) - CHUNKS) * 16)
                        parts = [slot[g][:, :, i_k, i, :] for i in range(2)]
                    last = multiply(k, parts, tiles3(acc_early), tiles3(acc_late))
                    if k % GROUP == GROUP - 1:
                        last.then_inc(s_group, 1)
                        step(*before, q)

            pe.wait_ge(s_w, 16 * 5)
            pe.wait_ge(s_const, 2)
            for q in range(LEAD):
                transpose_group(0, 0, q)
            pe.wait_ge(s_xtail, GROUPS)
            chunk0(0, True, False)
            with pe.Fori(1, CHUNKS - 1) as c:
                chunk0(c, False, False)
            chunk0(CHUNKS - 1, False, True)
            for s in range(1, LAST + 1):
                chunk(s, 0, (s - 1, CHUNKS - 1))
                with pe.Fori(1, CHUNKS) as c:
                    chunk(s, c, (s, c - 1))
            for k in range(3):
                step(LAST, CHUNKS - 1, k)


def kernel(**inputs):
    import concourse.bacc as bacc
    from concourse.bass_utils import run_bass_kernel_spmd as run

    a = {k: np.asarray(v) for k, v in inputs.items()}
    w = {f"{t}_W{i}": a[f"L0_gnn_{t}_W{i}"] for t in ("uv", "vu") for i in (1, 2, 3)}
    b = {f"{t}_b{i}": a[f"L0_gnn_{t}_b{i}"] for t in ("uv", "vu") for i in (1, 2, 3)}
    w.update(L1_WT=a["L1_gnn_W"].T, L2_WselfT=a["L2_gnn_W"][:, :FEAT].T, L2_WneighT=a["L2_gnn_W"][:, FEAT:].T,
             L3_W1=a["L3_gnn_W1"], L3_W2=a["L3_gnn_W2"])
    b.update(L1_b=a["L1_gnn_b"], L2_b=a["L2_gnn_b"])
    arrays = {
        "adj": np.ascontiguousarray(a["adj"]),
        "x": np.ascontiguousarray(a["x"]),
        "mats": np.stack([w[n] for n in MATS]),
        "cols": np.stack([b[n] for n in COLS], axis=1),
        "rowvecs": np.stack([b[n] for n in ROWVECS]),
        "filters": np.stack([np.ascontiguousarray(a[n].reshape(TILES, P).T) for n in ("L3_gnn_f1", "L3_gnn_f2")]),
        "alpha": np.ascontiguousarray(a["L1_gnn_alpha"].reshape(1, 1)),
    }
    nc = bacc.Bacc("TRN2", target_bir_lowering=False, num_devices=1)
    args = [nc.dram_tensor(n, v.shape, mybir.dt.from_np(v.dtype), kind="ExternalInput").ap() for n, v in arrays.items()]
    result = nc.dram_tensor("result", (NODES, FEAT), mybir.dt.float32, kind="ExternalOutput").ap()
    build(nc, *args, result)
    r = run(nc, [arrays], core_ids=[0])
    return r.results[0]["result"]
```

```python
import numpy as np
import concourse.bass as bass
from concourse import mybir
from contextlib import ExitStack

P = 128
NODES = 4096
FEAT = 128
TILES = NODES // P
CHUNK = 512
CHUNKS = NODES // CHUNK
ROWS = CHUNK // P
GROUP = 4
GROUPS = TILES // GROUP
GROUP_ENDS = range(GROUP - 1, TILES, GROUP)
LATE = TILES - GROUP
RESIDENT = 5
STREAMED = TILES - RESIDENT
SLOT = 3
SLOTS = STREAMED // SLOT
PAIR = 2 * P
PARTS = 4
PART = NODES // PARTS
PER_PART = GROUPS // PARTS
NAT = NODES * 2
ASM = STREAMED * PAIR
GUESTS = 2
LONE = SLOT - GUESTS
EARLY_GUESTS = NAT // (GUESTS * ROWS * PAIR)
BUFFERS = 4
BLOCK = ROWS * PAIR
REGION = max(2 * NAT + NODES + ASM, (GUESTS * CHUNKS + LONE + BUFFERS * SLOT) * BLOCK)
TAILS_AFTER = (1, 3, 5, 7)
SCALES_AFTER = 2
LEAD = 2
PIECES = ((0, 1), (1, 3), (3, 6), (6, 9))
VECTOR_MOVES = (1, 2, 3, 4, 5, 6, 7)
SCALAR_MOVES = tuple(q for q in range(GROUPS) if q not in VECTOR_MOVES)

EPS = 1e-5
SLOPE = 0.01
TOP = 14
SHRINK = NODES.bit_length() - 1
EXPONENT = 0x7F800000
MIRROR = float(254 << 23)
SMALLEST = 2.0 ** -111

STAGES = ["uv", "vu", "uv", "vu", "uv_norm", "conv1", "conv2", "filter1", "relu", "filter2", "out"]
LAST = len(STAGES) - 1
MLP = ("uv", "vu", "uv_norm")
CONV = ("conv1", "conv2")
NORM = ("uv_norm", "conv1", "conv2", "out")
RELOADED = ("uv_norm", "out")
MATS = ["uv_W1", "uv_W2", "uv_W3", "vu_W1", "vu_W2", "vu_W3", "L1_WT", "L2_WselfT", "L2_WneighT", "L3_W1", "L3_W2"]
COLS = ["uv_b1", "uv_b2", "vu_b1", "vu_b2"]
ROWVECS = ["uv_b3", "vu_b3", "L1_b", "L2_b"]


def nth(kinds, s, c):
    return CHUNKS * sum(STAGES[r] in kinds for r in range(s)) + c + 1


def everywhere(s, c):
    return CHUNKS * s + c + 1


def build(nc, adj, x, mats, cols, rowvecs, filters, alpha, out):
    f32, f16, bf16, i32 = mybir.dt.float32, mybir.dt.float16, mybir.dt.bfloat16, mybir.dt.int32
    ALU, ACT, AX = mybir.AluOpType, mybir.ActivationFunctionType, mybir.AxisListType
    AMAX = bass.bass_isa.ReduceOp.absmax

    adjT = nc.dram_tensor("adjT", (CHUNKS, SLOTS, P, ROWS * SLOT * PAIR), f16, kind="Internal").ap()
    x3_dram = nc.dram_tensor("x3", (TILES, P, FEAT), f32, kind="Internal").ap()
    adj_v = adj.rearrange("(t p) (h k) -> t h p k", p=P, h=PARTS)
    x_v = x.rearrange("(t p) f -> p t f", p=P)
    out_v = out.rearrange("(t p) f -> t p f", p=P)

    with ExitStack() as ctx:
        def sb(name, shape, dt):
            return ctx.enter_context(nc.sbuf_tensor(name, shape, dt))

        def bank(name):
            return ctx.enter_context(nc.psum_tensor(name, [P, CHUNK], f32))

        def sem(name):
            return ctx.enter_context(nc.semaphore(name))

        home = sb("home", [P, CHUNKS, ROWS, RESIDENT, 2, P], f16)
        region = sb("region", [P, REGION], f16)
        nat = [region[:, b * NAT:(b + 1) * NAT].bitcast(f32) for b in range(2)]
        nat_tail = [region[:, b * NAT:(b + 1) * NAT].rearrange("p (k two) -> p k two", two=2)[:, :, 0] for b in range(2)]
        nat_head = region[:, 2 * NAT:2 * NAT + NODES]
        asm = region[:, 2 * NAT + NODES:2 * NAT + NODES + ASM].rearrange("p (k h n) -> p k h n", h=2, n=P)
        guests = region[:, 0:GUESTS * CHUNKS * BLOCK].rearrange(
            "p (c j k h n) -> p c j k h n", c=CHUNKS, k=GUESTS, h=2, n=P)
        after_guests = GUESTS * CHUNKS * BLOCK
        lone = region[:, after_guests:after_guests + LONE * BLOCK].rearrange("p (j k h n) -> p j k h n", k=LONE, h=2, n=P)
        after_lone = after_guests + LONE * BLOCK
        slot_flat = [region[:, after_lone + b * SLOT * BLOCK:after_lone + (b + 1) * SLOT * BLOCK] for b in range(BUFFERS)]
        slot = [v.rearrange("p (j k h n) -> p j k h n", k=SLOT, h=2, n=P) for v in slot_flat]
        x_parts = sb("x_parts", [P, TILES, 2, FEAT], f16)
        x_f32 = sb("x_f32", [P, TILES, FEAT], f32)
        undo_row = sb("undo_row", [P, CHUNKS, CHUNK], bf16)
        mat = sb("mat", [P, len(MATS), FEAT], f32)
        col = sb("col", [P, len(COLS)], f32)
        vec = sb("vec", [P, len(ROWVECS), FEAT], f32)
        filt = sb("filt", [P, 2, TILES], f32)
        alpha_c = sb("alpha_c", [P, 1], f32)
        beta_c = sb("beta_c", [P, 1], f32)
        eps_c = sb("eps_c", [P, 1], f32)
        ident = sb("ident", [P, P], f32)
        ident16 = sb("ident16", [P, P], f16)
        ones = sb("ones", [P, P], f32)
        diag = sb("diag", [P, ROWS, P], f32)
        part_mean = sb("part_mean", [P, PARTS], f32)
        magnitudes = sb("magnitudes", [P, PART], bf16)
        row_mean = sb("row_mean", [P, 1], f32)
        row_exp = sb("row_exp", [P, 1], f32)
        row_undo = sb("row_undo", [P, ROWS], f32)
        chunk_undo = sb("chunk_undo", [P, ROWS], f32)
        row_scale = sb("row_scale", [P, ROWS], f32)
        part_row_sum = sb("part_row_sum", [P, ROWS, PARTS], f32)
        row_sum = sb("row_sum", [P, ROWS], f32)
        degree = sb("degree", [P, TILES], f32)
        nonzero = sb("nonzero", [P, TILES], f32)
        inv_degree = sb("inv_degree", [P, TILES], f32)
        chunk_max = sb("chunk_max", [P, CHUNKS], f32)
        part_max = sb("part_max", [P, 1], f32)
        all_max = sb("all_max", [P, 1], f32)
        x_exp = sb("x_exp", [P, 1], f32)
        x_scale = sb("x_scale", [P, 2, 2], f32)
        x_undo = sb("x_undo", [P, 2, 2], f32)
        early = sb("early", [P, CHUNK], f32)
        z = sb("z", [P, CHUNK], f32)
        biased = sb("biased", [P, CHUNK], f32)
        h1 = sb("h1", [P, CHUNK], f32)
        h2 = sb("h2", [P, CHUNK], f32)
        y = sb("y", [P, ROWS, FEAT], f32)
        ysum = biased[:, :].rearrange("p (j f) -> p j f", j=ROWS)
        stats = sb("stats", [P, ROWS, 6], f32)
        apart = sb("apart", [P, ROWS], f32)
        twice_mean = sb("twice_mean", [P, ROWS], f32)
        mean = sb("mean", [P, ROWS], f32)
        within = sb("within", [P, ROWS], f32)
        between = sb("between", [P, ROWS], f32)
        spread = sb("spread", [P, ROWS], f32)
        std = sb("std", [P, ROWS], f32)
        rstd = sb("rstd", [P, ROWS], f32)

        acc_early, acc_late = bank("acc_early"), bank("acc_late")
        turned = [ctx.enter_context(nc.psum_tensor(f"turned{i}", [P, 2 * CHUNK], f16)) for i in range(4)]
        m0, m1 = bank("m0"), bank("m1")

        s_x = [sem(f"x_half{i}_loaded") for i in range(2)]
        s_w = sem("weights_loaded")
        s_const = sem("constants_ready")
        s_ident = sem("identity_zeroed")
        s_nat = [[sem(f"nat{b}{h}_loaded") for h in range(PARTS)] for b in range(2)]
        s_stored = [sem(f"piece{i}_stored") for i in range(len(PIECES))]
        s_guests = sem("guests_loaded")
        s_lone = sem("lone_block_loaded")
        s_slot = [sem(f"buffer{b}_loaded") for b in range(BUFFERS)]
        s_slot_used = sem("slot_multiplied")
        s_pmean = sem("part_mean_ready")
        s_rmean = sem("row_mean_ready")
        s_rexp = sem("row_exponent_ready")
        s_rundo = sem("row_undo_ready")
        s_rscale = sem("row_scale_ready")
        s_nhead = sem("part_heads_ready")
        s_ntail = sem("part_tails_ready")
        s_turned = sem("blocks_transposed")
        s_smoved = sem("group_moved_by_scalar")
        s_vmoved = sem("group_moved_by_vector")
        s_diag = sem("diagonal_ready")
        s_bcast = sem("row_undo_broadcast")
        s_undo = sem("undo_row_ready")
        s_kept = sem("chunk_undo_kept")
        s_rsum = sem("row_sum_ready")
        s_deg = sem("degree_ready")
        s_setup = sem("setup_step")
        s_group = sem("group_multiplied")
        s_early = sem("early_read")
        s_zsum = sem("late_read")
        s_zalpha = sem("alpha_z_ready")
        s_z = sem("z_ready")
        s_mm1 = sem("layer1_multiplied")
        s_biased1 = sem("layer1_biased")
        s_h1 = sem("h1_ready")
        s_mm2 = sem("layer2_multiplied")
        s_biased2 = sem("layer2_biased")
        s_h2 = sem("h2_ready")
        s_xt = sem("x_transposed")
        s_xtc = sem("x_transposed_copied")
        s_lin = sem("linear_done")
        s_linread = sem("linear_read")
        s_y = sem("y_ready")
        s_ysum = sem("y_sum_ready")
        s_stats = sem("stats_ready")
        s_apart = sem("apart_ready")
        s_within = sem("within_ready")
        s_between = sem("between_ready")
        s_mv = sem("mean_and_spread_ready")
        s_std = sem("std_ready")
        s_rstd = sem("rstd_ready")
        s_new = sem("new_x_ready")
        s_cmax = sem("chunk_max_ready")
        s_hmax = sem("x_half_max_ready")
        s_pmax = sem("partition_max_ready")
        s_amax = sem("all_max_ready")
        s_xexp = sem("x_exponent_ready")
        s_xundo = sem("x_undo_ready")
        s_xscale = sem("x_scale_ready")
        s_xhead = sem("x_head_ready")
        s_xtail = sem("x_parts_ready")
        s_reload = sem("residual_reloaded")
        s_spill = sem("x3_spilled")
        s_out = sem("out_stored")

        block = ctx.enter_context(nc.Block())

        def m(name):
            return mat[:, MATS.index(name), :]

        def column(name):
            return col[:, COLS.index(name):COLS.index(name) + 1]

        def per_row(name):
            return vec[:, ROWVECS.index(name), :].unsqueeze(1).to_broadcast([P, ROWS, FEAT])

        def rows(c):
            return slice(c * ROWS, (c + 1) * ROWS) if isinstance(c, int) else bass.ds(c * ROWS, ROWS)

        def x_half(i):
            return slice(i * TILES // 2, (i + 1) * TILES // 2)

        def following(c, j, n):
            return c + (j + n) // ROWS, (j + n) % ROWS

        def slot_used(s, c, back, g):
            last = RESIDENT + SLOT * (g + 1) - 1
            if last in GROUP_ENDS:
                return s_group, s * (CHUNKS * GROUPS) + c * GROUPS + (back * GROUPS + last // GROUP + 1)
            own = [r for r in range(SLOTS) if RESIDENT + SLOT * (r + 1) - 1 not in GROUP_ENDS]
            per = len(own)
            return s_slot_used, s * (CHUNKS * per) + c * per + (own.index(g) + 1 + back * per - CHUNKS * per)

        def tiles3(psum):
            return psum[:, :].rearrange("p (j n) -> p j n", j=ROWS)

        def places(c, j, q):
            k0, k1 = GROUP * q, GROUP * (q + 1)
            if k0 < RESIDENT:
                n = min(k1, RESIDENT) - k0
                yield 0, n, home[:, c, j, k0:k0 + n, :, :]
            if k1 > RESIDENT:
                a = max(k0, RESIDENT)
                yield a - k0, k1 - a, asm[:, a - RESIDENT:k1 - RESIDENT, :, :]

        def moved(t, q):
            for done, groups in ((s_vmoved, VECTOR_MOVES), (s_smoved, SCALAR_MOVES)):
                if q in groups:
                    return done, t * len(groups) + groups.index(q) + 1

        def wait_moved(eng, t, q):
            eng.wait_ge(*moved(t, q))

        def move(eng, copy, c, j, q, moved):
            t = c * ROWS + j
            eng.wait_ge(s_turned, GROUPS * t + q + 1)
            if not (isinstance(t, int) and t == 0):
                blocks = range(max(GROUP * q, RESIDENT) - RESIDENT, GROUP * (q + 1) - RESIDENT)
                for i, (a, b) in enumerate(PIECES):
                    if set(blocks) & set(range(a * SLOT, b * SLOT)):
                        eng.wait_ge(s_stored[i], 16 * t)
            for a, n, dest in places(c, j, q):
                last = copy(dest.rearrange("p k h n -> p (k h n)"), turned[q % 4][:, a * PAIR:(a + n) * PAIR])
            last.then_inc(moved, 1)

        def x_count(s, late):
            return 1 if s == 0 else 2 * s + late

        def scale_at(table, s, late):
            late = late if s else 0
            return table[:, s % 2, late:late + 1]

        @block.sync
        def _(sp):
            def part(b, h):
                return nat[b][:, h * PART:(h + 1) * PART]

            for h in range(PARTS):
                sp.dma_start(part(0, h), adj_v[0, h]).then_inc(s_nat[0][h], 16)
            for i in range(2):
                sp.dma_start(x_f32[:, x_half(i), :], x_v[:, x_half(i), :]).then_inc(s_x[i], 16)
            for h in range(PARTS):
                sp.dma_start(part(1, h), adj_v[1, h]).then_inc(s_nat[1][h], 16)
            sp.dma_start(mat[:, :, :], mats.rearrange("m p f -> p m f")).then_inc(s_w, 16)
            sp.dma_start(col[:, :], cols).then_inc(s_w, 16)
            sp.dma_start(vec[:, :, :], rowvecs.unsqueeze(0).to_broadcast([P, len(ROWVECS), FEAT])).then_inc(s_w, 16)
            sp.dma_start(filt[:, :, :], filters.rearrange("a p t -> p a t")).then_inc(s_w, 16)
            sp.dma_start(alpha_c[:, :], alpha.to_broadcast([P, 1])).then_inc(s_w, 16)

            def load(c, j, h):
                sp.wait_ge(s_turned, GROUPS * (c * ROWS + j) + PER_PART * (h + 1))
                sp.dma_start(part(j % 2, h), adj_v[c * ROWS + j + 2, h]).then_inc(s_nat[j % 2][h], 16)

            def store(c, j, i):
                wait_moved(sp, c * ROWS + j, 2 * i + 1)
                a, b = PIECES[i]
                sp.dma_start(
                    adjT[c, a:b, :, j * SLOT * PAIR:(j + 1) * SLOT * PAIR].rearrange("g p e -> p g e"),
                    asm[:, a * SLOT:b * SLOT, :, :].rearrange("p (g k) h n -> p g (k h n)", k=SLOT),
                ).then_inc(s_stored[i], 16)

            def row_tile(c, j, more):
                for h in range(PARTS):
                    if more:
                        load(c, j, h)
                    if h:
                        store(c, j, h - 1)
                store(c, j, PARTS - 1)

            with sp.Fori(0, CHUNKS - 1) as c:
                for j in range(ROWS):
                    row_tile(c, j, True)

            def first_slot(c, i, n):
                return adjT[c, 0].rearrange("p (j k e) -> p j k e", j=ROWS, k=SLOT)[:, :, i:i + n, :]

            def load_guests(c):
                sp.dma_start(guests[:, c, :, :, :, :].rearrange("p j k h n -> p j k (h n)"),
                             first_slot(c, 0, GUESTS)).then_inc(s_guests, 16)

            def load_lone(c):
                sp.dma_start(lone.rearrange("p j k h n -> p j k (h n)"), first_slot(c, GUESTS, LONE)).then_inc(s_lone, 16)

            def load_slot(c, g):
                b = (g - 1) % BUFFERS
                sp.dma_start(slot_flat[b], adjT[c, g]).then_inc(s_slot[b], 16)

            def stream(s, c):
                sp.wait_ge(*slot_used(s, c, -1, 0))
                load_lone(c)
                for g in range(1, SLOTS):
                    sp.wait_ge(*(slot_used(s, c, 0, g - BUFFERS) if g > BUFFERS else slot_used(s, c, -1, g + BUFFERS)))
                    load_slot(c, g)

            for j in range(ROWS - 1):
                row_tile(CHUNKS - 1, j, j + 2 < ROWS)
            sp.wait_ge(s_turned, GROUPS * (TILES - 1))
            sp.wait_ge(s_stored[0], 16 * ROWS * EARLY_GUESTS)
            for c in range(EARLY_GUESTS):
                load_guests(c)
            for i in range(3):
                store(CHUNKS - 1, ROWS - 1, i)
            sp.wait_ge(s_turned, GROUPS * TILES)
            load_lone(0)
            sp.wait_ge(s_stored[1], 16 * ROWS)
            load_slot(0, 1)
            store(CHUNKS - 1, ROWS - 1, 3)
            sp.wait_ge(s_group, GROUPS * CHUNKS)
            for stored in s_stored:
                sp.wait_ge(stored, 16 * TILES)
            for g in range(2, SLOTS):
                if g > BUFFERS:
                    sp.wait_ge(*slot_used(1, 0, 0, g - BUFFERS))
                load_slot(0, g)
            with sp.Fori(1, EARLY_GUESTS) as c:
                stream(1, c)
            with sp.Fori(EARLY_GUESTS, CHUNKS) as c:
                load_guests(c)
                stream(1, c)
            with sp.Fori(2, LAST + 1) as s:
                with sp.Fori(0, CHUNKS) as c:
                    stream(s, c)

        @block.gpsimd
        def _(pool):
            nc.gpsimd.memset(ident[:, :], 0.0).then_inc(s_ident, 1)
            nc.gpsimd.memset(ones[:, :], 1.0)
            nc.gpsimd.memset(eps_c[:, :], EPS)
            pool.wait_ge(s_ident, 1)
            nc.gpsimd.affine_select(out=ident[:, :], in_=ident[:, :], compare_op=ALU.not_equal, fill=1.0, base=0,
                                    pattern=[[-1, P]], channel_multiplier=1).then_inc(s_const, 1)
            pool.wait_ge(s_const, 1)
            nc.gpsimd.tensor_copy(ident16[:, :], ident[:, :]).then_inc(s_const, 1)

            def reduce_max(s, late):
                pool.wait_ge(s_pmax, x_count(s, late))
                nc.gpsimd.partition_all_reduce(all_max[:, :], part_max[:, :], P, AMAX).then_inc(s_amax, 1)

            def reload(s, source):
                for c in range(CHUNKS):
                    pool.wait_ge(s_xtail, CHUNKS * s + c + 1)
                    if nth(RELOADED, s, c) > 1:
                        pool.wait_ge(s_reload, 16 * (nth(RELOADED, s, c) - 1))
                    pool.dma_start(x_f32[:, c * ROWS:(c + 1) * ROWS, :],
                                   source[:, c * ROWS:(c + 1) * ROWS, :]).then_inc(s_reload, 16)

            def write_rows(s, c, dest, done):
                pool.wait_ge(s_new, everywhere(s, c))
                pool.dma_start(dest[rows(c), :, :].rearrange("t p f -> p t f"), x_f32[:, rows(c), :]).then_inc(done, 16)

            reduce_max(0, 0)
            for s in range(LAST + 1):
                if STAGES[s] == "uv_norm":
                    reload(s, x_v)
                if STAGES[s] == "out":
                    pool.wait_ge(s_spill, 16 * CHUNKS)
                    reload(s, x3_dram.rearrange("t p f -> p t f"))
                for c in range(CHUNKS):
                    if STAGES[s] == "conv2":
                        write_rows(s, c, x3_dram, s_spill)
                    if STAGES[s] == "out":
                        write_rows(s, c, out_v, s_out)
                    if s < LAST and c >= CHUNKS - 2:
                        reduce_max(s + 1, int(c == CHUNKS - 1))
            pool.wait_ge(s_out, 16 * CHUNKS)

        @block.scalar
        def _(act):
            def row_magnitudes(c, j, h):
                t = c * ROWS + j
                act.wait_ge(s_nat[j % 2][h], 16 * (c * (ROWS // 2) + j // 2 + 1))
                if h == 0 and not (isinstance(t, int) and t == 0):
                    act.wait_ge(s_rmean, t)
                if h or not (isinstance(t, int) and t == 0):
                    act.wait_ge(s_pmean, PARTS * t + h)
                nc.scalar.activation(magnitudes[:, :], nat[j % 2][:, h * PART:(h + 1) * PART], ACT.Abs,
                                     scale=2.0 ** -SHRINK, accum_out=part_mean[:, h:h + 1]).then_inc(s_pmean, 1)

            def nat_heads(c, j, h):
                t = c * ROWS + j
                act.wait_ge(s_rscale, t + 1)
                if not (isinstance(t, int) and t == 0):
                    act.wait_ge(s_turned, GROUPS * (t - 1) + PER_PART * (h + 1))
                if j == 0 and h == 0 and not (isinstance(t, int) and t == 0):
                    act.wait_ge(s_rsum, c)
                nc.scalar.activation(nat_head[:, h * PART:(h + 1) * PART], nat[j % 2][:, h * PART:(h + 1) * PART],
                                     ACT.Copy, scale=row_scale[:, j:j + 1],
                                     accum_out=part_row_sum[:, j, h:h + 1]).then_inc(s_nhead, 1)

            def diagonal(c, j, first):
                act.wait_ge(s_rundo, c * ROWS + j + 1)
                if j == 0 and not first:
                    act.wait_ge(s_bcast, c)
                nc.scalar.activation(diag[:, j, :], ident[:, :], ACT.Copy,
                                     scale=row_undo[:, j:j + 1]).then_inc(s_diag, 1)

            def copy(dest, src):
                return nc.scalar.activation(dest, src, ACT.Copy)

            def read_early(s, c):
                act.wait_ge(s_group, GROUPS * everywhere(s, c) - 1)
                if s or not (isinstance(c, int) and c == 0):
                    act.wait_ge(s_zsum, everywhere(s, c) - 1)
                nc.scalar.activation(early[:, :], acc_early[:, :], ACT.Copy,
                                     scale=scale_at(x_undo, s, 0)).then_inc(s_early, 1)

            def hidden1(s, c):
                act.wait_ge(s_mm1, nth(MLP, s, c))
                nc.scalar.activation(biased[:, :], m0[:, :], ACT.Identity,
                                     bias=column(STAGES[s][:2] + "_b1")).then_inc(s_biased1, 1)

            def hidden2(s, c):
                act.wait_ge(s_mm2, nth(MLP, s, c))
                nc.scalar.activation(biased[:, :], m1[:, :], ACT.Identity,
                                     bias=column(STAGES[s][:2] + "_b2")).then_inc(s_biased2, 1)

            def after(s, c):
                if STAGES[s] in MLP:
                    hidden1(s, c)
                    hidden2(s, c)
                if STAGES[s] in CONV:
                    act.wait_ge(s_xt, nth(CONV, s, c))
                    act.wait_ge(s_lin, everywhere(s, c) - 1)
                    nc.scalar.activation(h1[:, :], m1[:, :], ACT.Copy,
                                         scale=scale_at(x_undo, s, int(isinstance(c, int)))).then_inc(s_xtc, 1)
                if STAGES[s] in NORM:
                    act.wait_ge(s_mv, nth(NORM, s, c))
                    nc.scalar.activation(std[:, :], spread[:, :], ACT.Sqrt, bias=eps_c[:, 0:1],
                                     scale=1.0 / FEAT).then_inc(s_std, 1)

            def x_head(s, b):
                act.wait_ge(s_xscale, x_count(s, int(b == GROUPS - 1)))
                if s:
                    act.wait_ge(s_group, GROUPS * CHUNKS * s - GROUPS + b + 1)
                nc.scalar.activation(x_parts[:, b * GROUP:(b + 1) * GROUP, 0, :], x_f32[:, b * GROUP:(b + 1) * GROUP, :],
                                     ACT.Copy, scale=scale_at(x_scale, s, int(b == GROUPS - 1))).then_inc(s_xhead, 1)

            for h in range(PARTS):
                row_magnitudes(0, 0, h)
            for h in range(PARTS - 1):
                nat_heads(0, 0, h)
            act.wait_ge(s_const, 1)
            diagonal(0, 0, True)

            def chunk0(c, first, final):
                for j in range(ROWS):
                    t1, t2 = following(c, j, 1), following(c, j, 2)
                    left = ROWS - 1 - j if final else ROWS
                    if j == 0 and not first:
                        read_early(0, c - 1)
                    for q in range(GROUPS):
                        if q in SCALAR_MOVES:
                            move(act, copy, c, j, q, s_smoved)
                        if first and j == 0 and q == 0:
                            row_magnitudes(0, 1, 0)
                            row_magnitudes(0, 1, 1)
                            for b in range(GROUPS):
                                x_head(0, b)
                                if b in (1, 3):
                                    row_magnitudes(0, 1, (b + 3) // 2)
                        if q % PER_PART == 0:
                            h = q // PER_PART - 1
                            if h < 0:
                                if left >= 1 and not (first and j == 0):
                                    row_magnitudes(*t1, PARTS - 1)
                                nat_heads(c, j, PARTS - 1)
                            else:
                                if left >= 1:
                                    nat_heads(*t1, h)
                                    if h == 0:
                                        diagonal(*t1, False)
                                if left >= 2:
                                    row_magnitudes(*t2, h)
                        if q == 1 and j == ROWS - 1:
                            act.wait_ge(s_bcast, c + 1)
                            copy(undo_row[:, c, :], m1[:, :]).then_inc(s_undo, 1)
                        if q == 1 and j == 1 and not first:
                            hidden1(0, c - 1)
                        if q == 1 and j == 2 and not first:
                            hidden2(0, c - 1)

            chunk0(0, True, False)
            act.wait_ge(s_w, 16 * 5)
            with act.Fori(1, CHUNKS - 1) as c:
                chunk0(c, False, False)
            chunk0(CHUNKS - 1, False, True)
            for b in range(GROUPS - 1):
                x_head(1, b)
            read_early(0, CHUNKS - 1)
            after(0, CHUNKS - 1)
            x_head(1, GROUPS - 1)

            for s in range(1, LAST + 1):
                with act.Fori(0, CHUNKS - 1) as c:
                    read_early(s, c)
                    after(s, c)
                if s < LAST:
                    for b in range(GROUPS - 1):
                        x_head(s + 1, b)
                read_early(s, CHUNKS - 1)
                after(s, CHUNKS - 1)
                if s < LAST:
                    x_head(s + 1, GROUPS - 1)

        @block.vector
        def _(dve):
            def power_of_two(largest, top, exponent, undo, scale, s_exp, s_und, s_sc, n):
                nc.vector.tensor_scalar(exponent.bitcast(i32), largest.bitcast(i32), EXPONENT, None,
                                        ALU.bitwise_and).then_inc(s_exp, 1)
                dve.wait_ge(s_exp, n)
                nc.vector.tensor_scalar(undo, exponent, SMALLEST, 2.0 ** -top, ALU.max, ALU.mult).then_inc(s_und, 1)
                dve.wait_ge(s_und, n)
                nc.vector.tensor_scalar(scale.bitcast(i32), undo.bitcast(i32), -1.0, MIRROR,
                                        ALU.mult, ALU.add).then_inc(s_sc, 1)

            def row_scales(c, j, first):
                t = c * ROWS + j
                dve.wait_ge(s_pmean, PARTS * (t + 1))
                nc.vector.tensor_reduce(row_mean[:, :], part_mean[:, :], axis=AX.X, op=ALU.add).then_inc(s_rmean, 1)
                dve.wait_ge(s_rmean, t + 1)
                if j == 0 and not first:
                    dve.wait_ge(s_diag, ROWS * c)
                power_of_two(row_mean[:, :], TOP - SHRINK, row_exp[:, :], row_undo[:, j:j + 1], row_scale[:, j:j + 1],
                             s_rexp, s_rundo, s_rscale, t + 1)

            def nat_tails(c, j, h):
                dve.wait_ge(s_nhead, PARTS * (c * ROWS + j) + h + 1)
                nc.vector.scalar_tensor_tensor(nat_tail[j % 2][:, h * PART:(h + 1) * PART],
                                               nat[j % 2][:, h * PART:(h + 1) * PART], row_scale[:, j:j + 1],
                                               nat_head[:, h * PART:(h + 1) * PART],
                                               ALU.mult, ALU.subtract).then_inc(s_ntail, 1)

            def sum_products(s, c):
                n = everywhere(s, c)
                dve.wait_ge(s_group, GROUPS * n)
                dve.wait_ge(s_early, n)
                nc.vector.scalar_tensor_tensor(z[:, :], acc_late[:, :], scale_at(x_undo, s, 1), early[:, :],
                                               ALU.mult, ALU.add).then_inc(s_zsum, 1)
                dve.wait_ge(s_zsum, n)
                if s or not (isinstance(c, int) and c == 0):
                    dve.wait_ge(s_lin, n - 1)
                if STAGES[s] != "conv1":
                    nc.vector.tensor_tensor(z[:, :], z[:, :], undo_row[:, c, :], ALU.mult).then_inc(s_z, 1)
                    return
                k = nth(("conv1",), s, c)
                nc.vector.scalar_tensor_tensor(z[:, :], z[:, :], alpha_c[:, 0:1], undo_row[:, c, :],
                                               ALU.mult, ALU.mult).then_inc(s_zalpha, 1)
                dve.wait_ge(s_zalpha, k)
                dve.wait_ge(s_xtc, k)
                nc.vector.scalar_tensor_tensor(z[:, :], h1[:, :], beta_c[:, 0:1], z[:, :],
                                               ALU.mult, ALU.add).then_inc(s_z, 1)

            def leaky(s, c, s_biased, h, s_h):
                dve.wait_ge(s_biased, nth(MLP, s, c))
                nc.vector.scalar_tensor_tensor(h[:, :], biased[:, :], SLOPE, biased[:, :],
                                               ALU.mult, ALU.max).then_inc(s_h, 1)

            def hidden(s, c):
                if STAGES[s] in MLP:
                    leaky(s, c, s_biased1, h1, s_h1)
                    leaky(s, c, s_biased2, h2, s_h2)

            def finish(s, c):
                kind = STAGES[s]
                n = everywhere(s, c)
                x_c = x_f32[:, rows(c), :]
                lin = tiles3(m0)
                dve.wait_ge(s_lin, n)
                if kind == "filter1":
                    dve.wait_ge(s_spill, 16 * CHUNKS)
                if kind in RELOADED:
                    dve.wait_ge(s_reload, 16 * nth(RELOADED, s, c))
                if kind in MLP:
                    nc.vector.tensor_tensor(y[:, :, :], lin, per_row(kind[:2] + "_b3"), ALU.add).then_inc(s_linread, 1)
                    dve.wait_ge(s_linread, n)
                    if kind == "uv_norm":
                        nc.vector.scalar_tensor_tensor(ysum[:, :, :], y[:, :, :], SLOPE, y[:, :, :],
                                                       ALU.mult, ALU.max).then_inc(s_y, 1)
                        dve.wait_ge(s_y, nth(("uv_norm", "conv1"), s, c))
                        nc.vector.tensor_tensor(y[:, :, :], ysum[:, :, :], x_c, ALU.add).then_inc(s_ysum, 1)
                    else:
                        nc.vector.scalar_tensor_tensor(x_c, y[:, :, :], SLOPE, y[:, :, :],
                                                       ALU.mult, ALU.max).then_inc(s_new, 1)
                elif kind == "conv1":
                    inv = inv_degree[:, rows(c)].unsqueeze(2).to_broadcast([P, ROWS, FEAT])
                    nc.vector.tensor_tensor(ysum[:, :, :], lin, inv, ALU.mult).then_inc(s_linread, 1)
                    dve.wait_ge(s_linread, n)
                    nc.vector.tensor_tensor(ysum[:, :, :], ysum[:, :, :], per_row("L1_b"), ALU.add).then_inc(s_y, 1)
                    dve.wait_ge(s_y, nth(("uv_norm", "conv1"), s, c))
                    nc.vector.scalar_tensor_tensor(y[:, :, :], ysum[:, :, :], 0.0, x_c,
                                                   ALU.max, ALU.add).then_inc(s_ysum, 1)
                elif kind == "conv2":
                    nc.vector.tensor_tensor(ysum[:, :, :], lin, per_row("L2_b"), ALU.add).then_inc(s_linread, 1)
                    dve.wait_ge(s_linread, n)
                    nc.vector.tensor_tensor(y[:, :, :], ysum[:, :, :], x_c, ALU.add).then_inc(s_ysum, 1)
                elif kind in ("filter1", "filter2"):
                    f = filt[:, int(kind == "filter2"), rows(c)].unsqueeze(2).to_broadcast([P, ROWS, FEAT])
                    nc.vector.tensor_tensor(x_c, lin, f, ALU.mult).then_inc(s_new, 1)
                elif kind == "relu":
                    nc.vector.tensor_scalar(x_c, lin, 0.0, None, ALU.max).then_inc(s_new, 1)
                else:
                    nc.vector.tensor_tensor(y[:, :, :], lin, x_c, ALU.add).then_inc(s_ysum, 1)
                if kind in NORM:
                    k = nth(NORM, s, c)
                    dve.wait_ge(s_ysum, k)
                    for j in range(ROWS):
                        last = nc.vector.bn_stats(stats[:, j, :], y[:, j, :])
                    last.then_inc(s_stats, 1)
                    dve.wait_ge(s_stats, k)
                    nc.vector.tensor_tensor(apart[:, :], stats[:, :, 1], stats[:, :, 4], ALU.subtract).then_inc(s_apart, 1)
                    nc.vector.tensor_tensor(twice_mean[:, :], stats[:, :, 1], stats[:, :, 4], ALU.add)
                    nc.vector.tensor_tensor(within[:, :], stats[:, :, 2], stats[:, :, 5], ALU.add).then_inc(s_within, 1)
                    dve.wait_ge(s_apart, k)
                    nc.vector.scalar_tensor_tensor(between[:, :], apart[:, :], FEAT / 4.0, apart[:, :],
                                                   ALU.mult, ALU.mult).then_inc(s_between, 1)
                    dve.wait_ge(s_within, k)
                    nc.vector.tensor_scalar(mean[:, :], twice_mean[:, :], 0.5, None, ALU.mult)
                    dve.wait_ge(s_between, k)
                    nc.vector.tensor_tensor(spread[:, :], within[:, :], between[:, :], ALU.add).then_inc(s_mv, 1)
                    dve.wait_ge(s_std, k)
                    nc.vector.reciprocal(rstd[:, :], std[:, :]).then_inc(s_rstd, 1)
                    dve.wait_ge(s_rstd, k)
                    for j in range(ROWS):
                        x_j = x_f32[:, c * ROWS + j, :]
                        last = nc.vector.tensor_scalar(x_j, y[:, j, :], mean[:, j:j + 1], rstd[:, j:j + 1],
                                                       ALU.subtract, ALU.mult)
                    last.then_inc(s_new, 1)
                if s < LAST:
                    dve.wait_ge(s_new, n)
                    nc.vector.tensor_reduce(chunk_max[:, bass.ds(c, 1)] if not isinstance(c, int) else
                                            chunk_max[:, c:c + 1], x_c, axis=AX.XY, op=ALU.max,
                                            apply_absolute_value=True).then_inc(s_cmax, 1)

            def x_half_largest(i):
                dve.wait_ge(s_x[i], 16)
                nc.vector.tensor_reduce(chunk_max[:, i:i + 1], x_f32[:, x_half(i), :], axis=AX.XY, op=ALU.max,
                                        apply_absolute_value=True).then_inc(s_hmax, 1)

            def x_largest():
                dve.wait_ge(s_hmax, 2)
                nc.vector.tensor_reduce(part_max[:, :], chunk_max[:, 0:2], axis=AX.X, op=ALU.max).then_inc(s_pmax, 1)

            def x_scales(s, late):
                n = x_count(s, late)
                if s:
                    dve.wait_ge(s_cmax, everywhere(s - 1, CHUNKS - 1 if late else CHUNKS - 2))
                    src = chunk_max[:, CHUNKS - 1:CHUNKS] if late else chunk_max[:, 0:CHUNKS - 1]
                    nc.vector.tensor_reduce(part_max[:, :], src, axis=AX.X, op=ALU.max).then_inc(s_pmax, 1)
                dve.wait_ge(s_amax, n)
                at = late if s else 0
                power_of_two(all_max[:, :], TOP, x_exp[:, :], x_undo[:, s % 2, at:at + 1], x_scale[:, s % 2, at:at + 1],
                             s_xexp, s_xundo, s_xscale, n)
                dve.wait_ge(s_xscale, n)

            def x_tail(s, b):
                dve.wait_ge(s_xhead, GROUPS * s + b + 1)
                nc.vector.scalar_tensor_tensor(x_parts[:, b * GROUP:(b + 1) * GROUP, 1, :],
                                               x_f32[:, b * GROUP:(b + 1) * GROUP, :],
                                               scale_at(x_scale, s, int(b == GROUPS - 1)),
                                               x_parts[:, b * GROUP:(b + 1) * GROUP, 0, :],
                                               ALU.mult, ALU.subtract).then_inc(s_xtail, 1)

            dve.wait_ge(s_const, 1)
            row_scales(0, 0, True)
            x_half_largest(0)
            nat_tails(0, 0, 0)
            x_half_largest(1)
            x_largest()
            nat_tails(0, 0, 1)
            x_scales(0, 0)

            def chunk0(c, first, final):
                for j in range(ROWS):
                    nxt = (c + (j + 1) // ROWS, (j + 1) % ROWS)
                    ahead = not (final and j == ROWS - 1)
                    for q in range(GROUPS):
                        if first and j == 0:
                            x_tail(0, q)
                        if q in VECTOR_MOVES:
                            move(dve, nc.vector.tensor_copy, c, j, q, s_vmoved)
                        if q in TAILS_AFTER:
                            h = TAILS_AFTER.index(q) + 2
                            if h < PARTS:
                                nat_tails(c, j, h)
                            elif ahead:
                                nat_tails(*nxt, h - PARTS)
                        if q == 1 and j == ROWS - 1:
                            nc.vector.tensor_copy(chunk_undo[:, :], row_undo[:, :]).then_inc(s_kept, 1)
                            dve.wait_ge(s_kept, c + 1)
                        if q == SCALES_AFTER and ahead:
                            row_scales(*nxt, False)
                        if q == SCALES_AFTER and j == ROWS - 1:
                            dve.wait_ge(s_nhead, PARTS * ROWS * (c + 1))
                            nc.vector.tensor_reduce(row_sum[:, :], part_row_sum[:, :, :], axis=AX.X,
                                                    op=ALU.add).then_inc(s_rsum, 1)
                            dve.wait_ge(s_rsum, c + 1)
                            nc.vector.tensor_tensor(degree[:, rows(c)], row_sum[:, :], chunk_undo[:, :],
                                                    ALU.mult).then_inc(s_deg, 1)
                            dve.wait_ge(s_deg, c + 1)
                        if q == 5 and j == 0 and not first:
                            dve.wait_ge(s_undo, c)
                            sum_products(0, c - 1)
                        if q == 4 and j == 1 and not first:
                            leaky(0, c - 1, s_biased1, h1, s_h1)
                        if q == 4 and j == 2 and not first:
                            leaky(0, c - 1, s_biased2, h2, s_h2)
                        if q == (2 if final else 6) and j == 3 and not first:
                            finish(0, c - 1)
                        if final and j == ROWS - 1:
                            if q == 4:
                                x_scales(1, 0)
                            if q > 4:
                                x_tail(1, q - 5)

            chunk0(0, True, False)
            dve.wait_ge(s_w, 16 * 5)
            with dve.Fori(1, CHUNKS - 1) as c:
                chunk0(c, False, False)
            chunk0(CHUNKS - 1, False, True)
            for b in range(GROUPS - 5, GROUPS - 1):
                x_tail(1, b)
            dve.wait_ge(s_undo, CHUNKS)
            sum_products(0, CHUNKS - 1)
            hidden(0, CHUNKS - 1)
            finish(0, CHUNKS - 1)
            x_scales(1, 1)
            x_tail(1, GROUPS - 1)

            steps = [0]

            def setup(instruction):
                steps[0] += 1
                instruction.then_inc(s_setup, 1)
                dve.wait_ge(s_setup, steps[0])

            dve.wait_ge(s_deg, CHUNKS)
            setup(nc.vector.tensor_scalar(beta_c[:, :], alpha_c[:, :], -1.0, 1.0, ALU.mult, ALU.add))
            setup(nc.vector.tensor_scalar(degree[:, :], degree[:, :], alpha_c[:, 0:1], beta_c[:, 0:1],
                                          ALU.mult, ALU.add))
            setup(nc.vector.tensor_scalar(nonzero[:, :], degree[:, :], 0.0, None, ALU.is_equal))
            setup(nc.vector.tensor_tensor(degree[:, :], degree[:, :], nonzero[:, :], ALU.add))
            setup(nc.vector.tensor_scalar(nonzero[:, :], nonzero[:, :], -1.0, 1.0, ALU.mult, ALU.add))
            setup(nc.vector.reciprocal(inv_degree[:, :], degree[:, :]))
            setup(nc.vector.tensor_tensor(inv_degree[:, :], inv_degree[:, :], nonzero[:, :], ALU.mult))

            for s in range(1, LAST + 1):
                with dve.Fori(0, CHUNKS - 1) as c:
                    sum_products(s, c)
                    hidden(s, c)
                    finish(s, c)
                if s < LAST:
                    x_scales(s + 1, 0)
                    for b in range(GROUPS - 1):
                        x_tail(s + 1, b)
                sum_products(s, CHUNKS - 1)
                hidden(s, CHUNKS - 1)
                finish(s, CHUNKS - 1)
                if s < LAST:
                    x_scales(s + 1, 1)
                    x_tail(s + 1, GROUPS - 1)

        @block.tensor
        def _(pe):
            def multiply(k, head_and_tail, early_to, late_to):
                to = early_to if k < LATE else late_to
                head, tail = head_and_tail
                first, last = k in (0, LATE), k in (LATE - 1, TILES - 1)
                nc.tensor.matmul(to, x_parts[:, k, 0, :], head, start=first, stop=False)
                nc.tensor.matmul(to, x_parts[:, k, 0, :], tail, start=False, stop=False)
                return nc.tensor.matmul(to, x_parts[:, k, 1, :], head, start=False, stop=last)

            def free_m0(s, c):
                if s or not (isinstance(c, int) and c == 0):
                    pe.wait_ge(s_new, everywhere(s, c) - 1)

            def step(s, c, k):
                kind = STAGES[s]
                if kind in MLP:
                    w = kind[:2]
                    if k == 0:
                        pe.wait_ge(s_z, everywhere(s, c))
                        free_m0(s, c)
                        nc.tensor.matmul(m0[:, :], m(w + "_W1"), z[:, :], start=True, stop=True).then_inc(s_mm1, 1)
                    if k == 1:
                        pe.wait_ge(s_h1, nth(MLP, s, c))
                        if s == 0:
                            pe.wait_ge(s_undo, c + 1)
                        nc.tensor.matmul(m1[:, :], m(w + "_W2"), h1[:, :], start=True, stop=True).then_inc(s_mm2, 1)
                    if k == 2:
                        pe.wait_ge(s_h2, nth(MLP, s, c))
                        for j in range(ROWS):
                            last = nc.tensor.matmul(m0[:, j * P:(j + 1) * P], h2[:, j * P:(j + 1) * P], m(w + "_W3"),
                                                    start=True, stop=True)
                        last.then_inc(s_lin, 1)
                    return
                if kind in CONV:
                    if k == 0:
                        for j in range(ROWS):
                            for i in range(2):
                                last = nc.tensor.matmul(m1[:, j * P:(j + 1) * P], x_parts[:, c * ROWS + j, i, :],
                                                        ident16[:, :], start=i == 0, stop=i == 1)
                        last.then_inc(s_xt, 1)
                    if k == 1:
                        pe.wait_ge(s_z, everywhere(s, c))
                        free_m0(s, c)
                        if kind == "conv2":
                            pe.wait_ge(s_xtc, nth(CONV, s, c))
                        for j in range(ROWS):
                            z_j, x_j, to = z[:, j * P:(j + 1) * P], h1[:, j * P:(j + 1) * P], m0[:, j * P:(j + 1) * P]
                            if kind == "conv1":
                                last = nc.tensor.matmul(to, z_j, m("L1_WT"), start=True, stop=True)
                            else:
                                nc.tensor.matmul(to, z_j, m("L2_WneighT"), start=True, stop=False)
                                last = nc.tensor.matmul(to, x_j, m("L2_WselfT"), start=False, stop=True)
                        last.then_inc(s_lin, 1)
                    return
                if k == 0:
                    pe.wait_ge(s_z, everywhere(s, c))
                    free_m0(s, c)
                    for j in range(ROWS):
                        z_j, to = z[:, j * P:(j + 1) * P], m0[:, j * P:(j + 1) * P]
                        if kind in ("relu", "out"):
                            last = nc.tensor.transpose(to, z_j, ident[:, :])
                        else:
                            last = nc.tensor.matmul(to, z_j, m("L3_W1" if kind == "filter1" else "L3_W2"),
                                                    start=True, stop=True)
                    last.then_inc(s_lin, 1)

            def transpose_group(c, j, q):
                t, h = c * ROWS + j, q // PER_PART
                pe.wait_ge(s_ntail, PARTS * t + h + 1)
                if q >= 4:
                    wait_moved(pe, t, q - 4)
                elif not (isinstance(t, int) and t == 0):
                    wait_moved(pe, t - 1, q + 4)
                for i in range(GROUP):
                    at = slice((GROUP * q + i) * P, (GROUP * q + i + 1) * P)
                    nc.tensor.transpose(turned[q % 4][:, i * PAIR:i * PAIR + P], nat_head[:, at], ident16[:, :])
                    last = nc.tensor.transpose(turned[q % 4][:, i * PAIR + P:(i + 1) * PAIR],
                                               nat_tail[j % 2][:, at], ident16[:, :])
                last.then_inc(s_turned, 1)

            def multiply_group(c, j, q, first):
                wait_moved(pe, c * ROWS + j, q)
                if j == 0 and first:
                    pe.wait_ge(s_xtail, q + 1)
                if j == 0 and q == 0 and not first:
                    pe.wait_ge(s_early, c)
                if j == 0 and q == GROUPS - 1 and not first:
                    pe.wait_ge(s_zsum, c)
                for a, n, src in places(c, j, q):
                    for i in range(n):
                        last = multiply(GROUP * q + a + i, (src[:, i, 0, :], src[:, i, 1, :]),
                                        acc_early[:, j * P:(j + 1) * P], acc_late[:, j * P:(j + 1) * P])
                if j == ROWS - 1:
                    last.then_inc(s_group, 1)

            def chunk0(c, first, final):
                for j in range(ROWS):
                    for q in range(GROUPS):
                        if q + LEAD < GROUPS:
                            transpose_group(c, j, q + LEAD)
                        elif j + 1 < ROWS:
                            transpose_group(c, j + 1, q + LEAD - GROUPS)
                        elif not final:
                            transpose_group(c + 1, 0, q + LEAD - GROUPS)
                        if q == 0 and j == ROWS - 1:
                            pe.wait_ge(s_diag, ROWS * (c + 1))
                            if not first:
                                pe.wait_ge(s_h2, c)
                            for i in range(ROWS):
                                last = nc.tensor.matmul(m1[:, i * P:(i + 1) * P], ones[:, :], diag[:, i, :],
                                                        start=True, stop=True)
                            last.then_inc(s_bcast, 1)
                        multiply_group(c, j, q, first)
                    if not first:
                        step(0, c - 1, j)

            def chunk(s, c, before):
                n = everywhere(s, c) - 1
                for k in range(TILES):
                    q = k // GROUP
                    if k % GROUP == 0 and isinstance(c, int):
                        pe.wait_ge(s_xtail, GROUPS * s + q + 1)
                    if k == 0:
                        pe.wait_ge(s_early, n)
                    if k == LATE:
                        pe.wait_ge(s_zsum, n)
                    g, i_k = divmod(k - RESIDENT, SLOT)
                    if k < RESIDENT:
                        where = home[:, c, :, k, :, :]
                    elif k < RESIDENT + GUESTS:
                        if s == 1 and i_k == 0:
                            pe.wait_ge(s_guests, 16 * (EARLY_GUESTS if isinstance(c, int) else c + 1))
                        where = guests[:, c, :, i_k, :, :]
                    elif g == 0:
                        if i_k == GUESTS:
                            pe.wait_ge(s_lone, (everywhere(s, c) - CHUNKS) * 16)
                        where = lone[:, :, i_k - GUESTS, :, :]
                    else:
                        turn, b = divmod(g - 1, BUFFERS)
                        if i_k == 0:
                            turns = (SLOTS - 1) // BUFFERS
                            pe.wait_ge(s_slot[b], (everywhere(s, c) - CHUNKS - 1) * (16 * turns) + 16 * (turn + 1))
                        where = slot[b][:, :, i_k, :, :]
                    last = multiply(k, [where[:, :, i, :] for i in range(2)], tiles3(acc_early), tiles3(acc_late))
                    if k >= RESIDENT and i_k == SLOT - 1 and k not in GROUP_ENDS:
                        last.then_inc(s_slot_used, 1)
                    if k % GROUP == GROUP - 1:
                        last.then_inc(s_group, 1)
                        step(*before, q)

            pe.wait_ge(s_const, 2)
            for q in range(LEAD):
                transpose_group(0, 0, q)
            chunk0(0, True, False)
            pe.wait_ge(s_w, 16 * 5)
            with pe.Fori(1, CHUNKS - 1) as c:
                chunk0(c, False, False)
            chunk0(CHUNKS - 1, False, True)
            for s in range(1, LAST + 1):
                chunk(s, 0, (s - 1, CHUNKS - 1))
                with pe.Fori(1, CHUNKS) as c:
                    chunk(s, c, (s, c - 1))
            for k in range(3):
                step(LAST, CHUNKS - 1, k)


def kernel(**inputs):
    import concourse.bacc as bacc
    from concourse.bass_utils import run_bass_kernel_spmd as run

    a = {k: np.asarray(v) for k, v in inputs.items()}
    w = {f"{t}_W{i}": a[f"L0_gnn_{t}_W{i}"] for t in ("uv", "vu") for i in (1, 2, 3)}
    b = {f"{t}_b{i}": a[f"L0_gnn_{t}_b{i}"] for t in ("uv", "vu") for i in (1, 2, 3)}
    w.update(L1_WT=a["L1_gnn_W"].T, L2_WselfT=a["L2_gnn_W"][:, :FEAT].T, L2_WneighT=a["L2_gnn_W"][:, FEAT:].T,
             L3_W1=a["L3_gnn_W1"], L3_W2=a["L3_gnn_W2"])
    b.update(L1_b=a["L1_gnn_b"], L2_b=a["L2_gnn_b"])
    arrays = {
        "adj": np.ascontiguousarray(a["adj"]),
        "x": np.ascontiguousarray(a["x"]),
        "mats": np.stack([w[n] for n in MATS]),
        "cols": np.stack([b[n] for n in COLS], axis=1),
        "rowvecs": np.stack([b[n] for n in ROWVECS]),
        "filters": np.stack([np.ascontiguousarray(a[n].reshape(TILES, P).T) for n in ("L3_gnn_f1", "L3_gnn_f2")]),
        "alpha": np.ascontiguousarray(a["L1_gnn_alpha"].reshape(1, 1)),
    }
    nc = bacc.Bacc("TRN2", target_bir_lowering=False, num_devices=1)
    args = [nc.dram_tensor(n, v.shape, mybir.dt.from_np(v.dtype), kind="ExternalInput").ap() for n, v in arrays.items()]
    result = nc.dram_tensor("result", (NODES, FEAT), mybir.dt.float32, kind="ExternalOutput").ap()
    build(nc, *args, result)
    r = run(nc, [arrays], core_ids=[0])
    return r.results[0]["result"]
```
